# Optimizing a Trainium2 kernel written in Bass

```python
import numpy as np
import jax
import jax.numpy as jnp

def _softmax(x, axis=-1):
    return jax.nn.softmax(x, axis=axis)

def _gelu(x):
    return jax.nn.gelu(x, approximate=True)

def _silu(x):
    return jax.nn.silu(x)

def _sigmoid(x):
    return jax.nn.sigmoid(x)

def _layernorm(x, axis=-1, eps=1e-05):
    m = jnp.mean(x, axis=axis, keepdims=True)
    v = jnp.var(x, axis=axis, keepdims=True)
    return (x - m) / jnp.sqrt(v + eps)

def _scatter_add(tgt, idx, src, axis=0):
    return tgt.at[idx].add(src)

def _segment_sum(src, seg, n):
    return jax.ops.segment_sum(src, seg, n)
kernel_name = 'mk_macaron_d2_jaxref_r8_ef179a'

def setup_inputs(seed: int=0):
    np.random.seed(seed)
    _w = jnp.asarray

    def _L0_attn_setup():
        import math
        import jax, jax.numpy as jnp
        import numpy as np
        EPS = 1e-06
        NEG = -1000000000.0

        def rms_norm(x):
            return x * jax.lax.rsqrt(jnp.mean(x * x, axis=-1, keepdims=True) + EPS)

        def apply_rope(x, cos, sin):
            d2 = x.shape[-1] // 2
            x1, x2 = (x[..., :d2], x[..., d2:])
            c = cos[None, None, :, :]
            s = sin[None, None, :, :]
            return jnp.concatenate([x1 * c - x2 * s, x2 * c + x1 * s], axis=-1)
        key = jax.random.key(seed)
        k1, k2, k3 = jax.random.split(key, 3)
        B, T, C = (2, 256, 128)
        H, D = (16, 64)
        dim_inner = H * D
        x = jax.random.normal(k1, (B, T, C), dtype=jnp.float32)
        w_qkv = jax.random.normal(k2, (3 * dim_inner, C), dtype=jnp.float32) * (1.0 / math.sqrt(C))
        w_out = jax.random.normal(k3, (C, dim_inner), dtype=jnp.float32) * (1.0 / math.sqrt(dim_inner))
        return {'x': x, 'w_qkv': w_qkv, 'w_out': w_out}
    _L0_attn_in = _L0_attn_setup()

    def _L0_ffn_setup():
        import jax, jax.numpy as jnp
        import numpy as np
        DIM = 128
        DEPTH = 2
        HEADS = 8
        DIM_HEAD = 64
        WINDOW = 64
        INNER = HEADS * DIM_HEAD
        HID = int(DIM * 4 * 2 / 3)
        B, N = (2, 1024)
        QK_SCALE = 8.0

        def shift_token(t):
            t1, t2 = jnp.split(t, 2, axis=-1)
            t2 = jnp.pad(t2, ((0, 0), (1, 0), (0, 0)))[:, :-1]
            return jnp.concatenate([t1, t2], axis=-1)

        def l2norm(t):
            return t / jnp.clip(jnp.linalg.norm(t, axis=-1, keepdims=True), 1e-12)

        def rotate_half(x):
            x1, x2 = jnp.split(x, 2, axis=-1)
            return jnp.concatenate([-x2, x1], axis=-1)

        def rotary_xpos(q, k):
            n = q.shape[-2]
            half_idx = jnp.arange(0, DIM_HEAD, 2, dtype=jnp.float32)
            inv_freq = 1.0 / 10000.0 ** (half_idx / DIM_HEAD)
            t = jnp.arange(n, dtype=jnp.float32)
            freqs = t[:, None] * inv_freq[None, :]
            freqs = jnp.concatenate([freqs, freqs], axis=-1)
            base = (half_idx + 0.4 * DIM_HEAD) / (1.4 * DIM_HEAD)
            power = (t - n // 2) / float(WINDOW // 2)
            scale = base[None, :] ** power[:, None]
            scale = jnp.concatenate([scale, scale], axis=-1)
            cos, sin = (jnp.cos(freqs), jnp.sin(freqs))
            q = q * cos * scale + rotate_half(q) * sin * scale
            k = k * cos / scale + rotate_half(k) * sin / scale
            return (q, k)

        def local_attention(q, k, v):
            b, h, n, d = q.shape
            w = n // WINDOW
            bq = q.reshape(b, h, w, WINDOW, d) * QK_SCALE
            bk = k.reshape(b, h, w, WINDOW, d)
            bv = v.reshape(b, h, w, WINDOW, d)

            def look_around(t):
                p = jnp.pad(t, ((0, 0), (0, 0), (1, 0), (0, 0), (0, 0)))
                return jnp.concatenate([p[:, :, :w], p[:, :, 1:]], axis=3)
            bk, bv = (look_around(bk), look_around(bv))
            bt = jnp.arange(n).reshape(w, WINDOW)
            btp = jnp.pad(bt, ((1, 0), (0, 0)), constant_values=-1)
            btk = jnp.concatenate([btp[:w], btp[1:]], axis=1)
            sim = jnp.einsum('bhwid,bhwjd->bhwij', bq, bk)
            i = bt[:, :, None]
            j = btk[:, None, :]
            mask = (i < j) | (i > j + WINDOW) | (j == -1)
            sim = jnp.where(mask, -jnp.finfo(sim.dtype).max, sim)
            attn = jax.nn.softmax(sim, axis=-1)
            out = jnp.einsum('bhwij,bhwjd->bhwid', attn, bv)
            return out.reshape(b, h, n, d)

        def _layer(x, wqkv, qs, ksc, wo, lg, lb, w1, b1, w2, b2):
            b, n, _ = x.shape
            h = shift_token(x)
            qkv = h @ wqkv
            q, k, v = jnp.split(qkv, 3, axis=-1)
            to_heads = lambda t: t.reshape(b, n, HEADS, DIM_HEAD).transpose(0, 2, 1, 3)
            q, k, v = (to_heads(q), to_heads(k), to_heads(v))
            q = l2norm(q) * qs
            k = l2norm(k) * ksc
            q, k = rotary_xpos(q, k)
            o = local_attention(q, k, v)
            o = o.transpose(0, 2, 1, 3).reshape(b, n, INNER)
            x = x + o @ wo
            h = shift_token(x)
            mu = h.mean(-1, keepdims=True)
            var = h.var(-1, keepdims=True)
            h = (h - mu) / jnp.sqrt(var + 1e-05) * lg + lb
            h = h @ w1 + b1
            a, g = jnp.split(h, 2, axis=-1)
            h = a * jax.nn.gelu(g, approximate=False)
            x = x + h @ w2 + b2
            return x
        key = jax.random.key(seed)
        ks = jax.random.split(key, 6)
        return {'x': jax.random.normal(ks[0], (B, N, DIM), jnp.float32), 'wqkv': jax.random.normal(ks[1], (DEPTH, DIM, 3 * INNER), jnp.float32) * 0.02, 'q_scale': jnp.ones((DEPTH, DIM_HEAD), jnp.float32), 'k_scale': jnp.ones((DEPTH, DIM_HEAD), jnp.float32), 'wo': jax.random.normal(ks[2], (DEPTH, INNER, DIM), jnp.float32) * 0.02, 'ln_g': jnp.ones((DEPTH, DIM), jnp.float32), 'ln_b': jnp.zeros((DEPTH, DIM), jnp.float32), 'w1': jax.random.normal(ks[3], (DEPTH, DIM, 2 * HID), jnp.float32) * 0.02, 'b1': jnp.zeros((DEPTH, 2 * HID), jnp.float32), 'w2': jax.random.normal(ks[4], (DEPTH, HID, DIM), jnp.float32) * 0.02, 'b2': jnp.zeros((DEPTH, DIM), jnp.float32)}
    _L0_ffn_in = _L0_ffn_setup()

    def _L1_attn_setup():
        import jax, jax.numpy as jnp
        import numpy as np
        NUM_HEADS = 16
        HIDDEN = 128
        HEAD_DIM = HIDDEN // NUM_HEADS
        B, L = (2, 256)
        key = jax.random.key(seed)
        ks = jax.random.split(key, 5)
        scale = 1.0 / np.sqrt(HIDDEN)
        return {'x': jax.random.normal(ks[0], (B, L, HIDDEN), dtype=jnp.float32), 'Wq': jax.random.normal(ks[1], (HIDDEN, HIDDEN), dtype=jnp.float32) * scale, 'Wk': jax.random.normal(ks[2], (HIDDEN, HIDDEN), dtype=jnp.float32) * scale, 'Wv': jax.random.normal(ks[3], (HIDDEN, HIDDEN), dtype=jnp.float32) * scale, 'Wo': jax.random.normal(ks[4], (HIDDEN, HIDDEN), dtype=jnp.float32) * scale}
    _L1_attn_in = _L1_attn_setup()

    def _L1_ffn_setup():
        import jax, jax.numpy as jnp
        import numpy as np
        B, T, C, H, E = (4, 256, 128, 256, 8)
        CAPACITY_FACTOR = 1.0
        key = jax.random.key(seed)
        ks = jax.random.split(key, 5)
        scale = 0.02
        return {'x': jax.random.normal(ks[0], (B, T, C), dtype=jnp.float32), 'Wg': jax.random.normal(ks[1], (E, C), dtype=jnp.float32) * scale, 'W1': jax.random.normal(ks[2], (E, H, C), dtype=jnp.float32) * scale, 'W2': jax.random.normal(ks[3], (E, C, H), dtype=jnp.float32) * scale, 'W3': jax.random.normal(ks[4], (E, H, C), dtype=jnp.float32) * scale}
    _L1_ffn_in = _L1_ffn_setup()
    _d = {'L0_attn_x': _L0_attn_in['x'], 'L0_attn_w_qkv': _L0_attn_in['w_qkv'], 'L0_attn_w_out': _L0_attn_in['w_out'], 'L0_ffn_wqkv': _L0_ffn_in['wqkv'], 'L0_ffn_q_scale': _L0_ffn_in['q_scale'], 'L0_ffn_k_scale': _L0_ffn_in['k_scale'], 'L0_ffn_wo': _L0_ffn_in['wo'], 'L0_ffn_ln_g': _L0_ffn_in['ln_g'], 'L0_ffn_ln_b': _L0_ffn_in['ln_b'], 'L0_ffn_w1': _L0_ffn_in['w1'], 'L0_ffn_b1': _L0_ffn_in['b1'], 'L0_ffn_w2': _L0_ffn_in['w2'], 'L0_ffn_b2': _L0_ffn_in['b2'], 'L1_attn_Wq': _L1_attn_in['Wq'], 'L1_attn_Wk': _L1_attn_in['Wk'], 'L1_attn_Wv': _L1_attn_in['Wv'], 'L1_attn_Wo': _L1_attn_in['Wo'], 'L1_ffn_Wg': _L1_ffn_in['Wg'], 'L1_ffn_W1': _L1_ffn_in['W1'], 'L1_ffn_W2': _L1_ffn_in['W2'], 'L1_ffn_W3': _L1_ffn_in['W3']}
    _x0 = _d['L0_attn_x']
    _d['L0_attn_x'] = jax.random.normal(jax.random.fold_in(jax.random.key(seed), 1), (4, 1024, 128), dtype=_x0.dtype)
    del _x0
    return _d

def reference(L0_attn_x, L0_attn_w_qkv, L0_attn_w_out, L0_ffn_wqkv, L0_ffn_q_scale, L0_ffn_k_scale, L0_ffn_wo, L0_ffn_ln_g, L0_ffn_ln_b, L0_ffn_w1, L0_ffn_b1, L0_ffn_w2, L0_ffn_b2, L1_attn_Wq, L1_attn_Wk, L1_attn_Wv, L1_attn_Wo, L1_ffn_Wg, L1_ffn_W1, L1_ffn_W2, L1_ffn_W3):

    def _L0_attn_ref(x, w_qkv, w_out):
        import math
        import jax, jax.numpy as jnp
        import numpy as np
        EPS = 1e-06
        NEG = -1000000000.0

        def rms_norm(x):
            return x * jax.lax.rsqrt(jnp.mean(x * x, axis=-1, keepdims=True) + EPS)

        def apply_rope(x, cos, sin):
            d2 = x.shape[-1] // 2
            x1, x2 = (x[..., :d2], x[..., d2:])
            c = cos[None, None, :, :]
            s = sin[None, None, :, :]
            return jnp.concatenate([x1 * c - x2 * s, x2 * c + x1 * s], axis=-1)
        H, D, window_size = (16, 64, 32)
        B, T, C = x.shape
        xn = rms_norm(x)
        qkv = xn @ w_qkv.T
        q, k, v = jnp.split(qkv, 3, axis=-1)
        q = q.reshape(B, T, H, D).transpose(0, 2, 1, 3)
        k = k.reshape(B, T, H, D).transpose(0, 2, 1, 3)
        v = v.reshape(B, T, H, D).transpose(0, 2, 1, 3)
        inv_freq = 1.0 / 10000.0 ** (jnp.arange(0, D, 2, dtype=jnp.float32) / D)
        freqs = jnp.outer(jnp.arange(T, dtype=jnp.float32), inv_freq)
        cos, sin = (jnp.cos(freqs), jnp.sin(freqs))
        q = apply_rope(q, cos, sin)
        k = apply_rope(k, cos, sin)
        scale = 1.0 / math.sqrt(D)
        attn = jnp.einsum('bhqd,bhkd->bhqk', q, k) * scale
        q_pos = jnp.arange(T)[:, None]
        k_pos = jnp.arange(T)[None, :]
        mask = (q_pos >= k_pos) & (q_pos - k_pos <= window_size)
        attn = jnp.where(mask[None, None], attn, NEG)
        attn = jax.nn.softmax(attn.astype(jnp.float32), axis=-1).astype(q.dtype)
        out = jnp.einsum('bhqk,bhkd->bhqd', attn, v)
        out = out.transpose(0, 2, 1, 3).reshape(B, T, H * D)
        return out @ w_out.T

    def _L0_ffn_ref(x, wqkv, q_scale, k_scale, wo, ln_g, ln_b, w1, b1, w2, b2):
        import jax, jax.numpy as jnp
        import numpy as np
        DIM = 128
        DEPTH = 2
        HEADS = 8
        DIM_HEAD = 64
        WINDOW = 64
        INNER = HEADS * DIM_HEAD
        HID = int(DIM * 4 * 2 / 3)
        B, N = (2, 1024)
        QK_SCALE = 8.0

        def shift_token(t):
            t1, t2 = jnp.split(t, 2, axis=-1)
            t2 = jnp.pad(t2, ((0, 0), (1, 0), (0, 0)))[:, :-1]
            return jnp.concatenate([t1, t2], axis=-1)

        def l2norm(t):
            return t / jnp.clip(jnp.linalg.norm(t, axis=-1, keepdims=True), 1e-12)

        def rotate_half(x):
            x1, x2 = jnp.split(x, 2, axis=-1)
            return jnp.concatenate([-x2, x1], axis=-1)

        def rotary_xpos(q, k):
            n = q.shape[-2]
            half_idx = jnp.arange(0, DIM_HEAD, 2, dtype=jnp.float32)
            inv_freq = 1.0 / 10000.0 ** (half_idx / DIM_HEAD)
            t = jnp.arange(n, dtype=jnp.float32)
            freqs = t[:, None] * inv_freq[None, :]
            freqs = jnp.concatenate([freqs, freqs], axis=-1)
            base = (half_idx + 0.4 * DIM_HEAD) / (1.4 * DIM_HEAD)
            power = (t - n // 2) / float(WINDOW // 2)
            scale = base[None, :] ** power[:, None]
            scale = jnp.concatenate([scale, scale], axis=-1)
            cos, sin = (jnp.cos(freqs), jnp.sin(freqs))
            q = q * cos * scale + rotate_half(q) * sin * scale
            k = k * cos / scale + rotate_half(k) * sin / scale
            return (q, k)

        def local_attention(q, k, v):
            b, h, n, d = q.shape
            w = n // WINDOW
            bq = q.reshape(b, h, w, WINDOW, d) * QK_SCALE
            bk = k.reshape(b, h, w, WINDOW, d)
            bv = v.reshape(b, h, w, WINDOW, d)

            def look_around(t):
                p = jnp.pad(t, ((0, 0), (0, 0), (1, 0), (0, 0), (0, 0)))
                return jnp.concatenate([p[:, :, :w], p[:, :, 1:]], axis=3)
            bk, bv = (look_around(bk), look_around(bv))
            bt = jnp.arange(n).reshape(w, WINDOW)
            btp = jnp.pad(bt, ((1, 0), (0, 0)), constant_values=-1)
            btk = jnp.concatenate([btp[:w], btp[1:]], axis=1)
            sim = jnp.einsum('bhwid,bhwjd->bhwij', bq, bk)
            i = bt[:, :, None]
            j = btk[:, None, :]
            mask = (i < j) | (i > j + WINDOW) | (j == -1)
            sim = jnp.where(mask, -jnp.finfo(sim.dtype).max, sim)
            attn = jax.nn.softmax(sim, axis=-1)
            out = jnp.einsum('bhwij,bhwjd->bhwid', attn, bv)
            return out.reshape(b, h, n, d)

        def _layer(x, wqkv, qs, ksc, wo, lg, lb, w1, b1, w2, b2):
            b, n, _ = x.shape
            h = shift_token(x)
            qkv = h @ wqkv
            q, k, v = jnp.split(qkv, 3, axis=-1)
            to_heads = lambda t: t.reshape(b, n, HEADS, DIM_HEAD).transpose(0, 2, 1, 3)
            q, k, v = (to_heads(q), to_heads(k), to_heads(v))
            q = l2norm(q) * qs
            k = l2norm(k) * ksc
            q, k = rotary_xpos(q, k)
            o = local_attention(q, k, v)
            o = o.transpose(0, 2, 1, 3).reshape(b, n, INNER)
            x = x + o @ wo
            h = shift_token(x)
            mu = h.mean(-1, keepdims=True)
            var = h.var(-1, keepdims=True)
            h = (h - mu) / jnp.sqrt(var + 1e-05) * lg + lb
            h = h @ w1 + b1
            a, g = jnp.split(h, 2, axis=-1)
            h = a * jax.nn.gelu(g, approximate=False)
            x = x + h @ w2 + b2
            return x
        for l in range(DEPTH):
            x = _layer(x, wqkv[l], q_scale[l], k_scale[l], wo[l], ln_g[l], ln_b[l], w1[l], b1[l], w2[l], b2[l])
        return x

    def _L1_attn_ref(x, Wq, Wk, Wv, Wo):
        import jax, jax.numpy as jnp
        import numpy as np
        NUM_HEADS = 16
        HIDDEN = 128
        HEAD_DIM = HIDDEN // NUM_HEADS
        B, L = (2, 256)
        b, l, _ = x.shape
        q = (x @ Wq.T).reshape(b, l, NUM_HEADS, HEAD_DIM)
        k = (x @ Wk.T).reshape(b, l, NUM_HEADS, HEAD_DIM)
        v = (x @ Wv.T).reshape(b, l, NUM_HEADS, HEAD_DIM)
        q = jax.nn.elu(q) + 1.0
        k = jax.nn.elu(k) + 1.0
        kv = jnp.einsum('blhd,blhe->blhde', k, v)
        kv_cumsum = jnp.cumsum(kv, axis=1)
        k_cumsum = jnp.cumsum(k, axis=1)
        out = jnp.einsum('blhd,blhde->blhe', q, kv_cumsum)
        normalizer = jnp.clip(jnp.einsum('blhd,blhd->blh', q, k_cumsum), 1e-06, None)
        out = out / normalizer[..., None]
        out = out.reshape(b, l, HIDDEN)
        return out @ Wo.T

    def _L1_ffn_ref(x, Wg, W1, W2, W3):
        import jax, jax.numpy as jnp
        import numpy as np
        B, T, C, H, E = (4, 256, 128, 256, 8)
        CAPACITY_FACTOR = 1.0
        b, t, c = x.shape
        e = Wg.shape[0]
        n = b * t
        capacity = max(1, int(CAPACITY_FACTOR * n / e))
        x_flat = x.reshape(n, c)
        scores = (x_flat @ Wg.T).T
        top_vals, token_idx = jax.lax.top_k(scores, capacity)
        token_w = jax.nn.softmax(top_vals, axis=-1)
        xg = x_flat[token_idx]
        h = jax.nn.silu(jnp.einsum('eic,ehc->eih', xg, W1)) * jnp.einsum('eic,ehc->eih', xg, W3)
        y = jnp.einsum('eih,ech->eic', h, W2) * token_w[..., None]
        out = jnp.zeros_like(x_flat).at[token_idx.reshape(-1)].add(y.reshape(-1, c))
        return out.reshape(b, t, c)
    x = L0_attn_x
    x = x + 0.5 * _L0_ffn_ref(_layernorm(x, axis=-1), L0_ffn_wqkv, L0_ffn_q_scale, L0_ffn_k_scale, L0_ffn_wo, L0_ffn_ln_g, L0_ffn_ln_b, L0_ffn_w1, L0_ffn_b1, L0_ffn_w2, L0_ffn_b2)
    x = x + _L0_attn_ref(_layernorm(x, axis=-1), L0_attn_w_qkv, L0_attn_w_out)
    x = x + 0.5 * _L0_ffn_ref(_layernorm(x, axis=-1), L0_ffn_wqkv, L0_ffn_q_scale, L0_ffn_k_scale, L0_ffn_wo, L0_ffn_ln_g, L0_ffn_ln_b, L0_ffn_w1, L0_ffn_b1, L0_ffn_w2, L0_ffn_b2)
    x = x + 0.5 * _L1_ffn_ref(_layernorm(x, axis=-1), L1_ffn_Wg, L1_ffn_W1, L1_ffn_W2, L1_ffn_W3)
    x = x + _L1_attn_ref(_layernorm(x, axis=-1), L1_attn_Wq, L1_attn_Wk, L1_attn_Wv, L1_attn_Wo)
    x = x + 0.5 * _L1_ffn_ref(_layernorm(x, axis=-1), L1_ffn_Wg, L1_ffn_W1, L1_ffn_W2, L1_ffn_W3)
    return x

_drawn_inputs = setup_inputs


def setup_inputs(seed=0):
    import zlib

    import numpy as np

    out = dict(_drawn_inputs(seed))
    spreads = {'L0_ffn_q_scale': (1.0, 0.6),
     'L0_ffn_k_scale': (1.0, 0.6),
     'L0_ffn_ln_g': (1.0, 0.6),
     'L0_ffn_ln_b': (0.0, 0.8),
     'L0_ffn_b1': (0.0, 0.8),
     'L0_ffn_b2': (0.0, 0.1)}
    factors = {'L0_ffn_wqkv': 3.159,
     'L0_ffn_wo': 3.176,
     'L0_ffn_w1': 5.334,
     'L0_ffn_w2': 5.233,
     'L1_attn_Wq': 51.352,
     'L1_attn_Wk': 22.234,
     'L1_ffn_Wg': 64.0,
     'L1_ffn_W1': 64.0,
     'L1_ffn_W2': 64.0,
     'L1_ffn_W3': 64.0}
    for name, (base, spread) in spreads.items():
        noise = np.random.default_rng([zlib.crc32(name.encode()), seed]).standard_normal(out[name].shape)
        drawn = base * np.exp(spread * noise) if base else spread * noise
        out[name] = jnp.asarray(drawn.astype(out[name].dtype))
    for name, factor in factors.items():
        out[name] = (out[name] * factor).astype(out[name].dtype)
    return out
```

```python
from contextlib import ExitStack

import concourse.bass as bass
from concourse import mybir

ALU = mybir.AluOpType
ACT = mybir.ActivationFunctionType
AX = mybir.AxisListType
F32 = mybir.dt.float32
BF16 = mybir.dt.bfloat16
I32 = mybir.dt.int32
U32 = mybir.dt.uint32
RMAX = bass.bass_isa.ReduceOp.max

P = 128
BATCH = 4
SEQ = 1024
C = 128
NT = BATCH * SEQ // P
TPB = SEQ // P
HD = 64
BQ = 64
HG = 8
GW = HG * HD
DEPTH = 2
HID = 341
HC = 3
LAST = HID - 2 * P
LH, LD = 16, 8
EX = 8
EH = 256
CAP = BATCH * SEQ // EX
SG = CAP // P
AHEAD = 4
SEARCH = 17
QKV_L0 = 3 * GW
STAGES = 6


class Unit:

    def __init__(self, T, c, U, base):
        self.tile = T + c // U
        self.parity = (c // U) % 2
        self.group = c % U
        self.count = base + U * T + c

    def done(self, back=0):
        return self.count + 1 - back


def pipeline(eng, U, units, base, step, stages=3):
    def at(T, c, has):
        step(*[Unit(T, c - d, U, base) if has[d] else None for d in range(stages)])

    peel = 4 if U == 1 and (base == 0 or stages == 4) else 2
    for i in range(peel * U):
        at(0, i, [i >= d for d in range(stages)])
    with eng.Fori(peel, units // U, 2) as T:
        T = T.with_bounds(min_val=peel, max_val=units // U - 2)
        for c in range(2 * U):
            at(T, c, [True] * stages)
    for c in range(stages - 1):
        at(units // U, c, [d > c for d in range(stages)])


def bass_macaron(nc, x_in, wqkv, qsc, ksc, wo, lng, lnb, w1, b1, w2, awqkv, awout,
                 lwqkv, lwo, wg, ew1, ew3, ew2,
                 rope_a, rope_b, arope, mask_w, mask_s, ident, shift, carry, tri, ones, keep,
                 rowmask, tril, blockm, iota, iota4, tokhi, toklo, scanm, out):
    ctx = ExitStack()
    with ctx:
        def sb(name, shape, dt=F32):
            return ctx.enter_context(nc.sbuf_tensor(name, shape, dt))

        def sem(name):
            return ctx.enter_context(nc.semaphore(name))

        psF = ctx.enter_context(nc.psum_tensor("psF", [P, 3, 512], F32))
        psS = ctx.enter_context(nc.psum_tensor("psS", [P, 2, 512], F32))
        psP = ctx.enter_context(nc.psum_tensor("psP", [P, 2, 512], F32))
        psO = ctx.enter_context(nc.psum_tensor("psO", [P, 512], F32))

        X = sb("X", [P, NT, C])
        Z = sb("Z", [P, NT, C])
        idt = sb("idt", [P, P])
        idb = sb("idb", [P, P], BF16)
        keep_sb = sb("keep_sb", [P, NT])
        one = sb("one", [P, 1])
        epsln = sb("epsln", [P, 1])
        epsrms = sb("epsrms", [P, 1])
        rnbias = sb("rnbias", [P, 1])
        st = sb("st", [P, NT, 6])
        mean = sb("mean", [P, NT])
        var = sb("var", [P, NT])
        tmpa = sb("tmpa", [P, NT])
        tmpb = sb("tmpb", [P, NT])
        rstd = sb("rstd", [P, NT])
        ybuf = sb("ybuf", [P, 2, 2 * P])

        load_done = sem("load_done")
        konst = sem("konst")
        st_done = sem("st_done")
        ln_step = sem("ln_step")
        ln_var = sem("ln_var")
        ln_bias = sem("ln_bias")
        ln_act = sem("ln_act")
        stored = sem("stored")
        n_load = [0]
        n_ln = [0]
        n_lnact = [0]
        n_store = [0]
        n_prep = [0]
        prep = sem("prep")
        prep_mm = sem("prep_mm")
        n_pmm = [0]

        def fetch(sp, pairs):
            if n_load[0]:
                sp.wait_ge(load_done, n_load[0])
            for dst, src in pairs:
                sp.dma_start(dst, src).then_inc(load_done, 16)
                n_load[0] += 16

        def start_loads(pairs):
            with nc.Block() as block:
                @block.sync
                def _(sp):
                    fetch(sp, pairs)

        def arrive():
            with nc.Block() as block:
                @block.sync
                def _(sp):
                    sp.wait_ge(load_done, n_load[0])

        with nc.Block() as block:
            @block.vector
            def _(dve):
                dve.memset(one[:], 1.0).then_inc(konst, 1)
                dve.memset(epsln[:], 1e-5).then_inc(konst, 1)
                dve.memset(epsrms[:], 1e-6).then_inc(konst, 1)
                dve.memset(rnbias[:], 8.0 * 0.6931471805599453).then_inc(konst, 1)
                dve.wait_ge(konst, 4)

        start_loads([(X[:], x_in.rearrange("(t p) c -> p t c", p=P)), (idt[:], ident), (keep_sb[:], keep)])
        arrive()
        with nc.Block() as block:
            @block.vector
            def _(dve):
                dve.tensor_copy(idb[:], idt[:]).then_inc(konst, 1)

        def layernorm(src, dst, rms=False, ahead=()):
            b = n_ln[0]
            with nc.Block() as block:
                @block.sync
                def _(sp):
                    fetch(sp, ahead)

                @block.vector
                def _(dve):
                    with dve.Fori(0, NT, 16) as T:
                        T = T.with_bounds(min_val=0, max_val=NT - 16)
                        for u in range(16):
                            last = dve.bn_stats(st[:, T + u, :], src[:, T + u, :])
                        last.then_inc(st_done, 1)
                    dve.wait_ge(st_done, (b + 1) * (NT // 16))
                    dve.tensor_tensor(mean[:], st[:, :, 1], st[:, :, 4], ALU.add).then_inc(ln_step, 1)
                    dve.tensor_tensor(tmpa[:], st[:, :, 1], st[:, :, 4], ALU.subtract).then_inc(ln_step, 1)
                    dve.tensor_tensor(var[:], st[:, :, 2], st[:, :, 5], ALU.add).then_inc(ln_step, 1)
                    dve.wait_ge(ln_step, 8 * b + 3)
                    dve.tensor_scalar(mean[:], mean[:], 0.5, None, ALU.mult).then_inc(ln_step, 1)
                    dve.tensor_tensor(tmpb[:], tmpa[:], tmpa[:], ALU.mult).then_inc(ln_step, 1)
                    dve.tensor_scalar(var[:], var[:], 1.0 / C, None, ALU.mult).then_inc(ln_step, 1)
                    dve.wait_ge(ln_step, 8 * b + 6)
                    dve.scalar_tensor_tensor(var[:], tmpb[:], 0.25, var[:], ALU.mult, ALU.add).then_inc(ln_var, 1)
                    if rms:
                        dve.wait_ge(ln_act, n_lnact[0] + 2)
                        dve.tensor_tensor(tmpb[:], rstd[:], rstd[:], ALU.mult).then_inc(ln_step, 1)
                        dve.wait_ge(ln_step, 8 * b + 7)
                        dve.tensor_tensor(tmpb[:], tmpb[:], var[:], ALU.mult).then_inc(ln_step, 1)
                        dve.wait_ge(ln_act, n_lnact[0] + 4)
                        dve.tensor_tensor(rstd[:], rstd[:], tmpb[:], ALU.mult).then_inc(ln_var, 1)
                        dve.wait_ge(ln_var, LNV[0] + 2)
                    else:
                        dve.nop().then_inc(ln_step, 2)
                        dve.wait_ge(ln_act, n_lnact[0] + 2)
                    nc.vector.scalar_tensor_tensor(tmpa[:], mean[:], -1.0, rstd[:], ALU.mult, ALU.mult).then_inc(ln_bias, 1)
                    with dve.Fori(0, NT, 16) as T:
                        T = T.with_bounds(min_val=0, max_val=NT - 16)
                        for u in range(16):
                            if u % 2 == 0:
                                dve.tensor_scalar(dst[:, T + u, :], src[:, T + u, :], mean[:, bass.ds(T + u, 1)],
                                                  rstd[:, bass.ds(T + u, 1)], ALU.subtract, ALU.mult)

                @block.scalar
                def _(act):
                    act.preload_act_table_set("natural_log_exp_and_others")
                    act.wait_ge(ln_var, LNV[0] + 1)
                    act.activation(tmpa[:], var[:], ACT.Ln, bias=epsln[:]).then_inc(ln_act, 1)
                    act.wait_ge(ln_act, n_lnact[0] + 1)
                    act.activation(rstd[:], tmpa[:], ACT.Exp, scale=-0.5).then_inc(ln_act, 1)
                    if rms:
                        act.wait_ge(ln_step, 8 * b + 8)
                        act.activation(tmpa[:], tmpb[:], ACT.Ln, bias=epsrms[:]).then_inc(ln_act, 1)
                        act.wait_ge(ln_act, n_lnact[0] + 3)
                        act.activation(tmpb[:], tmpa[:], ACT.Exp, scale=-0.5).then_inc(ln_act, 1)
                    act.wait_ge(ln_bias, n_ln[0] + 1)
                    with act.Fori(0, NT, 16) as T:
                        T = T.with_bounds(min_val=0, max_val=NT - 16)
                        for u in range(1, 16, 2):
                            act.activation(dst[:, T + u, :], src[:, T + u, :], ACT.Identity,
                                           bias=tmpa[:, bass.ds(T + u, 1)], scale=rstd[:, bass.ds(T + u, 1)])
            n_ln[0] += 1
            n_lnact[0] += 4 if rms else 2
            LNV[0] += 2 if rms else 1

        LNV = [0]

        hT = sb("hT", [P, 2, P + 1])
        FX = ExitStack()

        def fb(name, shape, dt=F32):
            return FX.enter_context(nc.sbuf_tensor(name, shape, dt))

        sq = fb("sq", [P, 2 * GW])
        ss = fb("ss", [P, 2 * HG])
        lns = fb("lns", [P, 2 * HG])
        rn = fb("rn", [P, 2 * HG])
        qn = fb("qn", [P, 2, HG, HD])
        t1 = fb("t1", [P, 2, HG, HD])
        t2 = fb("t2", [P, 2, HG, HD])
        qk = fb("qk", [P, 2, HG, HD])
        qT = fb("qT", [P, 4, P])
        kT = fb("kT", [P, 2, 4, BQ + P])
        V = fb("V", [P, 2, 2, HG, HD + 1])
        VA = fb("VA", [P, 2, 2, HG, HD + 1])
        prob = fb("prob", [P, 2, 4, P])
        probT = fb("probT", [P, 2, 4, P])
        osb = fb("osb", [P, HG, HD])
        oT = fb("oT", [P, 4, P])
        negmax = fb("negmax", [P, 2, 4])
        rec = fb("rec", [P, 2, 4])
        comb = fb("comb", [P, TPB, 2, 2, HD])
        mask = fb("mask", [P, NT, P], BF16)
        WA = fb("WA", [P, 6 * GW])
        WO = fb("WO", [P, 8, C])
        H = fb("H", [P, NT, C])
        W1 = fb("W1", [P, 2 * HC, P])
        W1g = fb("W1g", [P, 2 * HC, P])
        b1c = fb("b1c", [P, 2 * HC])
        b1f = fb("b1f", [P, 2 * HC])
        W2 = fb("W2", [P, HC, C])
        lg = fb("lg", [P, 1])
        lb = fb("lb", [P, 1])
        shm = fb("shm", [P, P])
        cam = fb("cam", [P, P])
        qkrow = fb("qkrow", [P, 2, HD])

        WINDOWED_ONLY = ("hT_dve", "sq", "ss", "ssm", "ln", "rn", "qn")
        SIGNALS = (
            "ybuf", "hT_t", "hT_act", "hT_dve", "qk_mm", "v_mm", "sq", "ss", "ln", "rn", "qn", "t1", "t2", "t2_last",
            "qk", "k_sum", "qk_t", "qT", "kprev", "kT", "s0", "s1", "nm0", "nm1", "e0", "e1", "pt0", "pt1", "ptc0",
            "ptc1", "o0", "o1", "rec0", "rec1", "on0", "on1", "oT_t", "oT", "y", "res", "v", "va", "ssm")
        A_windowed = {k: sem("w_" + k) for k in SIGNALS}
        A_sliding = {k: sem("s_" + k) for k in SIGNALS if k not in WINDOWED_ONLY}
        n_unit = {1: 0, 2: 0}

        with nc.Block() as block:
            @block.vector
            def _(dve):
                dve.memset(kT[:], 0.0)
                dve.memset(V[:], 1.0)
                dve.memset(VA[:], 1.0)
                dve.memset(hT[:], 0.0)

        def attention(U, norm, shifted, dst):
            A = A_windowed if U == 1 else A_sliding
            base = n_unit[U]
            units = U * NT
            wq = WA[:, 0:3 * U * GW].rearrange("p (a g n) -> p a g n", a=3, g=U)
            with nc.Block() as block:
                @block.gpsimd
                def _(pool):
                    def step(f, n, m, k):
                        if m is not None:
                            g = m.group
                            if not (isinstance(m.tile, int) and m.tile == 0):
                                pool.wait_ge(A["s1"], m.done(U))
                            nc.gpsimd.tensor_tensor(
                                kT[:, g, :, 0:BQ], kT[:, g, :, P:P + BQ],
                                one[:].unsqueeze(2).to_broadcast([P, 4, BQ]), ALU.mult).then_inc(A["kprev"], 1)
                        if n is not None:
                            if norm:
                                pool.wait_ge(A["qn"], n.done())
                                if m is not None:
                                    pool.wait_ge(A["k_sum"], m.done())
                                for a, h in ((0, 0), (0, 1), (1, 0)):
                                    last = nc.gpsimd.tensor_tensor(
                                        t2[:, a, :, 32 * h:32 * h + 32], qn[:, a, :, 32 - 32 * h:64 - 32 * h],
                                        comb[:, n.tile & 7 if not isinstance(n.tile, int) else n.tile % TPB, 1, a,
                                             32 * h:32 * h + 32].unsqueeze(1).to_broadcast([P, HG, 32]), ALU.mult)
                                last.then_inc(A["t2"], 1)
                            pool.wait_ge(A["t2"], n.done())
                            pool.wait_ge(A["t1"], n.done())
                            if m is not None:
                                pool.wait_ge(A["qk_t"], m.done())
                            nc.gpsimd.tensor_tensor(qk[:, 0], t1[:, 0], t2[:, 0], ALU.add).then_inc(A["qk"], 1)

                    pipeline(pool, U, units, base, step, stages=4)

                @block.scalar
                def _(act):
                    act.preload_act_table_set("natural_log_exp_and_others")

                    def exps(m, q):
                        act.wait_ge(A[f"nm{q}"], m.done())
                        if not first(m):
                            act.wait_ge(A[f"pt{q}"], m.done(1))
                        for s in range(4):
                            last = nc.scalar.activation(prob[:, q, s, :],
                                                        psS[:, q, s * P:(s + 1) * P],
                                                        ACT.Exp, bias=negmax[:, q, s:s + 1])
                        last.then_inc(A[f"e{q}"], 1)

                    def probT_copy(m, q):
                        act.wait_ge(A[f"pt{q}"], m.done())
                        if not first(m):
                            act.wait_ge(A[f"o{q}"], m.done(1))
                        nc.scalar.copy(probT[:, q].rearrange("p s n -> p (s n)"), psP[:, q, :]).then_inc(A[f"ptc{q}"], 1)

                    def first(m):
                        return m is not None and isinstance(m.count, int) and m.count == base

                    def step(f, n, m, k):
                        if m is not None:
                            act.wait_ge(A["qk_t"], m.done())
                            if not first(m):
                                act.wait_ge(A["s1"], m.done(1))
                            nc.scalar.copy(qT[:].rearrange("p a n -> p (a n)"), psS[:, 0, :]).then_inc(A["qT"], 1)
                            act.wait_ge(A["v_mm"], m.done())
                            if not (isinstance(m.count, int) and m.count - base < 2):
                                act.wait_ge(A["o1"], m.done(2))
                            v = psF[:, 2, :].rearrange("p (h d) -> p h d", d=HD)
                            nc.scalar.copy(V[:, m.parity, m.group, :, 0:HD], v)
                            nc.scalar.copy(VA[BQ:P, m.parity, m.group, :, 0:HD], v[0:P - BQ]).then_inc(A["v"], 1)
                            if not (isinstance(m.tile, int) and m.tile == 0):
                                act.wait_ge(A["v"], m.done(U))
                            nc.scalar.copy(VA[0:BQ, m.parity, m.group, :, 0:HD],
                                           V[P - BQ:P, 1 - m.parity, m.group, :, 0:HD]).then_inc(A["va"], 1)
                        if f is not None:
                            par = f.group if U == 2 else f.parity
                            act.wait_ge(A["hT_t"], f.done())
                            if m is not None:
                                act.wait_ge(A["v_mm"], m.done())
                            if shifted:
                                if n is not None:
                                    act.wait_ge(A["hT_dve"], n.done())
                                nc.scalar.copy(hT[64:128, par, 1:P + 1], psP[64:128, 1, 0:P]).then_inc(A["hT_act"], 1)
                            else:
                                nc.scalar.copy(hT[:, par, 0:P], psP[:, 1, 0:P]).then_inc(A["hT_act"], 1)
                        if n is not None and norm:
                            act.wait_ge(A["ssm"], n.done())
                            nc.scalar.activation(lns[:], ss[:], ACT.Ln, scale=65536.0).then_inc(A["ln"], 1)
                            act.wait_ge(A["ln"], n.done())
                            if m is not None:
                                act.wait_ge(A["qn"], m.done())
                            nc.scalar.activation(rn[:], lns[:], ACT.Exp, scale=-0.5, bias=rnbias[:]).then_inc(A["rn"], 1)
                        if m is not None:
                            exps(m, 0)
                            exps(m, 1)
                            probT_copy(m, 0)
                            probT_copy(m, 1)
                        if f is not None and norm:
                            act.wait_ge(A["qk_mm"], f.done())
                            if n is not None:
                                act.wait_ge(A["ss"], n.done())
                            nc.scalar.activation(sq[:], psF[:, 0:2, :].rearrange("p b n -> p (b n)"),
                                                 ACT.Square).then_inc(A["sq"], 1)

                    pipeline(act, U, units, base, step, stages=4)

                @block.vector
                def _(dve):
                    def neg_max(m, q):
                        dve.wait_ge(A[f"s{q}"], m.done())
                        if not first(m):
                            dve.wait_ge(A[f"e{q}"], m.done(1))
                        nc.vector.tensor_reduce(negmax[:, q, :], psS[:, q, :].rearrange("p (s n) -> p s n", n=P),
                                                AX.X, ALU.max, negate=True).then_inc(A[f"nm{q}"], 1)

                    def first(m):
                        return m is not None and isinstance(m.count, int) and m.count == base

                    def normalise(m, q):
                        dve.wait_ge(A[f"o{q}"], m.done())
                        o = psO[:, 0:4 * (HD + 1)].rearrange("p (s d) -> p s d", d=HD + 1)
                        nc.vector.reciprocal(rec[:, q, :], o[:, :, HD]).then_inc(A[f"rec{q}"], 1)
                        dve.wait_ge(A[f"rec{q}"], m.done())
                        if q == 0 and not first(m):
                            dve.wait_ge(A["oT_t"], m.done(1))
                        nc.vector.tensor_tensor(osb[:, q:HG:2, :], o[:, :, 0:HD], rec[:, q, :].unsqueeze(2)
                                                .to_broadcast([P, 4, HD]), ALU.mult).then_inc(A[f"on{q}"], 1)

                    def position(n):
                        return n.tile & 7 if not isinstance(n.tile, int) else n.tile % TPB

                    def cosines(n, m, src):
                        if m is not None:
                            dve.wait_ge(A["qk"], m.done())
                            dve.wait_ge(A["k_sum"], m.done())
                        nc.vector.tensor_tensor(t1[:], src[:], comb[:, position(n), 0].unsqueeze(2)
                                                .to_broadcast([P, 2, HG, HD]), ALU.mult).then_inc(A["t1"], 1)

                    def step(f, n, m, k):
                        if f is not None:
                            if n is not None:
                                dve.wait_ge(A["hT_t"], n.done())
                            nc.vector.tensor_scalar(ybuf[:, 0, 0:P], Z[:, f.tile, :], 1.0, None,
                                                    ALU.mult).then_inc(A["ybuf"], 1)
                        if m is not None:
                            dve.wait_ge(A["qk_t"], m.done())
                            dve.wait_ge(A["kprev"], m.done())
                            nc.vector.tensor_copy(kT[:, m.group, :, BQ:BQ + P],
                                                  psS[:, 1, :].rearrange("p (a n) -> p a n", n=P)).then_inc(A["kT"], 1)
                        if k is not None:
                            normalise(k, 1)
                        if n is not None and not norm:
                            dve.wait_ge(A["qk_mm"], n.done())
                            if m is not None:
                                dve.wait_ge(A["qk"], m.done())
                                dve.wait_ge(A["k_sum"], m.done())
                            src = psF[:, 0:2, :].rearrange("p b (h d) -> p b h d", d=HD)
                            for h in range(2):
                                for a in range(2):
                                    last = nc.vector.tensor_tensor(
                                        t2[:, a, :, 32 * h:32 * h + 32], src[:, a, :, 32 - 32 * h:64 - 32 * h],
                                        comb[:, position(n), 1, a, 32 * h:32 * h + 32].unsqueeze(1).to_broadcast([P, HG, 32]),
                                        ALU.mult)
                            last.then_inc(A["t2"], 1)
                        if n is not None and norm:
                            dve.wait_ge(A["sq"], n.done())
                            if m is not None:
                                dve.wait_ge(A["ln"], m.done())
                            nc.vector.tensor_reduce(ss[:], sq[:].rearrange("p (h d) -> p h d", d=HD), AX.X,
                                                    ALU.add).then_inc(A["ss"], 1)
                            dve.wait_ge(A["ss"], n.done())
                            nc.vector.tensor_scalar(ss[:], ss[:], 1e-24, None, ALU.max).then_inc(A["ssm"], 1)
                        if f is not None and shifted:
                            par = f.parity
                            dve.wait_ge(A["hT_t"], f.done())
                            if m is not None:
                                dve.wait_ge(A["v_mm"], m.done())
                            nc.vector.tensor_copy(hT[0:64, par, 0:P], psP[0:64, 1, 0:P])
                            if n is not None:
                                dve.wait_ge(A["hT_act"], n.done())
                            nc.vector.tensor_tensor(hT[64:128, par, 0:1], hT[64:128, 1 - par, P:P + 1],
                                                    keep_sb[64:128, bass.ds(f.tile, 1)], ALU.mult).then_inc(A["hT_dve"], 1)
                        if m is not None:
                            neg_max(m, 0)
                        if k is not None:
                            dve.wait_ge(A["oT_t"], k.done())
                            nc.vector.tensor_copy(oT[:].rearrange("p a n -> p (a n)"), psP[:, 0, :]).then_inc(A["oT"], 1)
                        if n is not None and norm:
                            dve.wait_ge(A["rn"], n.done())
                            if m is not None:
                                dve.wait_ge(A["t2"], m.done())
                            nc.vector.tensor_tensor(qn[:], psF[:, 0:2, :].rearrange("p b (h d) -> p b h d", d=HD),
                                                    rn[:].rearrange("p (b h) -> p b h", b=2).unsqueeze(3)
                                                    .to_broadcast([P, 2, HG, HD]), ALU.mult).then_inc(A["qn"], 1)
                            dve.wait_ge(A["qn"], n.done())
                        if n is not None and not norm:
                            cosines(n, m, psF[:, 0:2, :].rearrange("p b (h d) -> p b h d", d=HD))
                        if m is not None:
                            neg_max(m, 1)
                        if n is not None and norm:
                            cosines(n, m, qn)
                        if k is not None:
                            dve.wait_ge(A["y"], k.done())
                            nc.vector.tensor_tensor(dst[:, k.tile, :], dst[:, k.tile, :], psO[:, 0:C],
                                                    ALU.add).then_inc(A["res"], 1)
                        if n is not None:
                            if norm:
                                nc.vector.tensor_tensor(t2[:, 1, :, 32:64], qn[:, 1, :, 0:32],
                                                        comb[:, position(n), 1, 1, 32:64].unsqueeze(1)
                                                        .to_broadcast([P, HG, 32]), ALU.mult).then_inc(A["t2_last"], 1)
                                dve.wait_ge(A["t2_last"], n.done())
                            dve.wait_ge(A["t2"], n.done())
                            dve.wait_ge(A["t1"], n.done())
                            if m is not None:
                                dve.wait_ge(A["qk_t"], m.done())
                            nc.vector.tensor_tensor(qk[:, 1], t1[:, 1], t2[:, 1], ALU.add).then_inc(A["k_sum"], 1)
                        if m is not None:
                            normalise(m, 0)

                    pipeline(dve, U, units, base, step, stages=4)

                @block.tensor
                def _(pe):
                    def first(m):
                        return m is not None and isinstance(m.count, int) and m.count == base

                    def scores(m, q):
                        nc.tensor.matmul(psS[:, q, :].rearrange("p (s n) -> p s n", n=P), idb[:],
                                         mask[:, m.tile, :].unsqueeze(1).to_broadcast([P, 4, P]),
                                         start=True, stop=False, skip_group_check=True)
                        for s in range(4):
                            for blk in range(2):
                                r = blk * BQ
                                last = nc.tensor.matmul(psS[r:r + BQ, q, s * P:(s + 1) * P],
                                                        qT[64 * q:64 * q + 64, s, r:r + BQ],
                                                        kT[64 * q:64 * q + 64, m.group, s, r:r + P],
                                                        start=False, stop=True, skip_group_check=True,
                                                        tile_position=(64 * q, r))
                        last.then_inc(A[f"s{q}"], 1)

                    def prob_turn(m, q):
                        pe.wait_ge(A[f"e{q}"], m.done())
                        for s in range(4):
                            last = nc.tensor.transpose(psP[:, q, s * P:(s + 1) * P], prob[:, q, s, :], idt[:])
                        last.then_inc(A[f"pt{q}"], 1)

                    def values(m, q):
                        pe.wait_ge(A[f"ptc{q}"], m.done())
                        for s in range(4):
                            for blk in range(2):
                                r = blk * BQ
                                v = V if blk else VA
                                last = nc.tensor.matmul(psO[r:r + BQ, s * (HD + 1):(s + 1) * (HD + 1)],
                                                        probT[:, q, s, r:r + BQ], v[:, m.parity, m.group, 2 * s + q, :],
                                                        start=True, stop=True, tile_position=(0, r))
                        last.then_inc(A[f"o{q}"], 1)

                    def hT_ready(f):
                        pe.wait_ge(A["hT_act"], f.done())
                        if shifted:
                            pe.wait_ge(A["hT_dve"], f.done())

                    def step(f, n, m, k):
                        if m is not None:
                            pe.wait_ge(A["qk"], m.done())
                            pe.wait_ge(A["k_sum"], m.done())
                            if k is not None:
                                pe.wait_ge(A["e1"], k.done())
                            for a in range(2):
                                for c in range(4):
                                    last = nc.tensor.transpose(psS[:, a, c * P:(c + 1) * P],
                                                               qk[:, a, 2 * c:2 * c + 2, :].rearrange("p h d -> p (h d)"), idt[:])
                            last.then_inc(A["qk_t"], 1)
                        if k is not None:
                            pe.wait_ge(A["on0"], k.done())
                            values(k, 1)
                        if f is not None:
                            pe.wait_ge(A["ybuf"], f.done())
                            if k is None and n is not None:
                                hT_ready(n)
                            nc.tensor.transpose(psP[:, 1, 0:P], ybuf[:, 0, 0:P], idt[:]).then_inc(A["hT_t"], 1)
                        if m is not None:
                            pe.wait_ge(A["qT"], m.done())
                            pe.wait_ge(A["kT"], m.done())
                            scores(m, 0)
                        if k is not None:
                            pe.wait_ge(A["on1"], k.done())
                            for c in range(4):
                                last = nc.tensor.transpose(psP[:, 0, c * P:(c + 1) * P],
                                                           osb[:, 2 * c:2 * c + 2, :].rearrange("p h d -> p (h d)"), idt[:])
                            last.then_inc(A["oT_t"], 1)
                        if m is not None:
                            scores(m, 1)
                        if n is not None:
                            par = n.group if U == 2 else n.parity
                            if m is not None:
                                pe.wait_ge(A["v"], m.done())
                            nc.tensor.matmul(psF[:, 2, :], hT[:, par, 0:P], wq[:, 2, n.group, :],
                                             start=True, stop=True).then_inc(A["v_mm"], 1)
                        if k is not None:
                            pe.wait_ge(A["oT"], k.done())
                            for c in range(4):
                                last = nc.tensor.matmul(psO[:, 0:C], oT[:, c, :], WO[:, 4 * k.group + c, :],
                                                        start=(c == 0), stop=(c == 3))
                            last.then_inc(A["y"], 1)
                        if m is not None:
                            prob_turn(m, 0)
                        if f is not None:
                            hT_ready(f)
                            par = f.group if U == 2 else f.parity
                            if n is not None:
                                pe.wait_ge(A["qn"] if norm else A["t1"], n.done())
                            for a in range(2):
                                last = nc.tensor.matmul(psF[:, a, :], hT[:, par, 0:P], wq[:, a, f.group, :],
                                                        start=True, stop=True)
                            last.then_inc(A["qk_mm"], 1)
                        if m is not None:
                            prob_turn(m, 1)
                            pe.wait_ge(A["v"], m.done())
                            pe.wait_ge(A["va"], m.done())
                            if k is not None:
                                pe.wait_ge(A["res"], k.done())
                            values(m, 0)

                    pipeline(pe, U, units, base, step, stages=4)
            n_unit[U] += units

        gl = fb("gl", [P, 2, HC, 2 * P])
        uT = fb("uT", [P, 2, HC, 2 * P])
        yT = fb("yT", [P, 2, 2 * P])
        B = {k: sem("b_" + k) for k in ("ybuf", "t", "yT", "up", "gelu", "u", "down", "res", "sh", "init", "h1")}
        n_b = [0]
        n_sh = [0]
        n_bi = [0]

        def shift_tokens():
            banks = [psF[:, 0, :], psF[:, 1, :], psF[:, 2, :], psO[:, :]]
            s0 = n_sh[0]
            with nc.Block() as block:
                @block.tensor
                def _(pe):
                    for b in range(BATCH):
                        t = TPB * b
                        nc.tensor.matmul(banks[b][:, :], shm[:], Z[:, t:t + TPB, 64:128], start=True, stop=False)
                        nc.tensor.matmul(banks[b][:, 64:512], cam[:], Z[:, t:t + TPB - 1, 64:128],
                                         start=False, stop=True).then_inc(B["sh"], 1)

                @block.scalar
                def _(act):
                    for b in range(BATCH):
                        act.wait_ge(B["sh"], s0 + b + 1)
                        nc.scalar.copy(H[:, TPB * b:TPB * b + TPB, 64:128],
                                       banks[b].rearrange("p (t c) -> p t c", c=64))

                @block.vector
                def _(dve):
                    nc.vector.tensor_copy(H[:, :, 0:64], Z[:, :, 0:64])
            n_sh[0] += BATCH

        def feed_forward():
            base = n_b[0]
            units = NT // 2
            i0 = n_bi[0]
            n_bi[0] += 1
            sets = [[psF[:, 0, :], psF[:, 1, :], psF[:, 2, :]], [psS[:, 0, :], psS[:, 1, :], psP[:, 0, :]]]
            turn = psP[:, 1, :]

            with nc.Block() as block:
                @block.vector
                def _(dve):
                    nc.vector.memset(uT[:], 1.0)

            def gated(st_, c, which):
                if c < 2:
                    return st_[which][:, c * 256:(c + 1) * 256]
                return st_[2][:, which * 256:(which + 1) * 256]

            with nc.Block() as block:
                @block.gpsimd
                def _(pool):
                    def step(n, m, k):
                        if n is not None:
                            if not (isinstance(n.count, int) and n.count - base < 2):
                                pool.wait_ge(B["t"], n.done(2))
                            nc.gpsimd.tensor_copy(ybuf[:, n.parity, :].rearrange("p (t c) -> p t c", c=C),
                                                  H[:, bass.ds(2 * n.tile, 2), :]).then_inc(B["ybuf"], 1)
                    pipeline(pool, 1, units, base, step)

                @block.tensor
                def _(pe):
                    def step(n, m, k):
                        if n is not None:
                            pe.wait_ge(B["ybuf"], n.done())
                            if m is not None:
                                pe.wait_ge(B["yT"], m.done())
                            for j in range(2):
                                last = nc.tensor.transpose(turn[:, j * P:(j + 1) * P], ybuf[:, n.parity, j * P:(j + 1) * P], idt[:])
                            last.then_inc(B["t"], 1)
                        if m is not None:
                            pe.wait_ge(B["yT"], m.done())
                            if not (isinstance(m.count, int) and m.count - base < 2):
                                pe.wait_ge(B["u"], m.done(2))
                            for c in range(HC):
                                for which in (1, 0):
                                    last = nc.tensor.matmul(gated(sets[m.parity], c, which), W1g[:, which * HC + c, :],
                                                            yT[:, m.parity, :], start=True, stop=True)
                            last.then_inc(B["up"], 1)
                        if k is not None:
                            pe.wait_ge(B["u"], k.done())
                            if not (isinstance(k.count, int) and k.count == base):
                                pe.wait_ge(B["res"], k.done(1))
                            for j in range(2):
                                for c in range(HC):
                                    last = nc.tensor.matmul(psO[:, j * C:(j + 1) * C], uT[:, k.parity, c, j * P:(j + 1) * P],
                                                            W2[:, c, :], start=(c == 0), stop=(c == HC - 1))
                            last.then_inc(B["down"], 1)
                    pipeline(pe, 1, units, base, step)

                @block.scalar
                def _(act):
                    def step(n, m, k):
                        if n is not None:
                            act.wait_ge(B["t"], n.done())
                            if not (isinstance(n.count, int) and n.count - base < 2):
                                act.wait_ge(B["up"], n.done(2))
                            nc.scalar.copy(yT[:, n.parity, :], turn[:, 0:2 * P]).then_inc(B["yT"], 1)
                        if m is not None:
                            act.wait_ge(B["up"], m.done())
                            if not (isinstance(m.count, int) and m.count - base < 2):
                                act.wait_ge(B["u"], m.done(2))
                            for c in range(HC):
                                last = nc.scalar.activation(gl[:, m.parity, c, :], gated(sets[m.parity], c, 1), ACT.Gelu,
                                                            bias=b1f[:, HC + c:HC + c + 1])
                            last.then_inc(B["gelu"], 1)
                    pipeline(act, 1, units, base, step)

                @block.vector
                def _(dve):
                    def step(n, m, k):
                        if m is not None:
                            dve.wait_ge(B["gelu"], m.done())
                            if not (isinstance(m.count, int) and m.count - base < 2):
                                dve.wait_ge(B["down"], m.done(2))
                            for c in range(HC):
                                r = P if c < HC - 1 else LAST
                                last = nc.vector.scalar_tensor_tensor(
                                    uT[0:r, m.parity, c, :], gated(sets[m.parity], c, 0)[0:r, :], b1f[0:r, c:c + 1],
                                    gl[0:r, m.parity, c, :], ALU.add, ALU.mult)
                            last.then_inc(B["u"], 1)
                        if k is not None:
                            dve.wait_ge(B["down"], k.done())
                            z = Z[:, bass.ds(2 * k.tile, 2), :]
                            nc.vector.tensor_tensor(z, z, psO[:, 0:2 * C].rearrange("p (t c) -> p t c", c=C),
                                                    ALU.add).then_inc(B["res"], 1)
                    pipeline(dve, 1, units, base, step)
            n_b[0] += units

        def windowed_loads(l):
            return ([(WA[:, 0:QKV_L0], wqkv[l]), (WO[:, 0:4, :], wo[l].rearrange("(a p) n -> p a n", p=P)),
                         (comb[:], rope_a), (mask[:], mask_w), (W1[:], w1[l].rearrange("p (a n) -> p a n", n=P)),
                         (b1c[:], b1[l]),
                         (lg[:], lng[l].rearrange("(p a) -> p a", a=1)), (lb[:], lnb[l].rearrange("(p a) -> p a", a=1)),
                         (qkrow[:, 0, :], qsc[l:l + 1, :].to_broadcast([P, HD])),
                         (qkrow[:, 1, :], ksc[l:l + 1, :].to_broadcast([P, HD]))])

        def windowed_prep(l):
            arrive()
            with nc.Block() as block:
                @block.sync
                def _(sp):
                    fetch(sp, [(W2[:], w2[l].rearrange("(a p) n -> p a n", p=P)), (shm[:], shift), (cam[:], carry)])

                @block.vector
                def _(dve):
                    nc.vector.tensor_scalar(W1g[:], W1[:], lg[:], None, ALU.mult)
                    for a in range(2):
                        nc.vector.tensor_tensor(comb[:, :, 0, a, :], comb[:, :, 0, a, :],
                                                qkrow[:, a, :].unsqueeze(1).to_broadcast([P, TPB, HD]), ALU.mult)
                        for h in range(2):
                            nc.vector.tensor_tensor(comb[:, :, 1, a, 32 * h:32 * h + 32], comb[:, :, 1, a, 32 * h:32 * h + 32],
                                                    qkrow[:, a, 32 - 32 * h:64 - 32 * h].unsqueeze(1).to_broadcast([P, TPB, 32]), ALU.mult)
                    dve.wait_ge(prep_mm, n_pmm[0] + 1)
                    nc.vector.tensor_tensor(b1f[:], b1c[:], psO[:, 0:2 * HC], ALU.add)

                @block.tensor
                def _(pe):
                    for c in range(2 * HC):
                        last = nc.tensor.matmul(psO[:, c:c + 1], W1[:, c, :], lb[:], start=True, stop=True)
                    last.then_inc(prep_mm, 1)
            n_pmm[0] += 1

        def axpy_half():
            with nc.Block() as block:
                @block.vector
                def _(dve):
                    nc.vector.scalar_tensor_tensor(X[:].rearrange("p t c -> p (t c)"), Z[:].rearrange("p t c -> p (t c)"), 0.5,
                                                   X[:].rearrange("p t c -> p (t c)"), ALU.mult, ALU.add)

        def sliding_loads():
            return ([(WA[:], awqkv), (WO[:], awout.rearrange("(a p) n -> p a n", p=P)),
                         (comb[:], arope), (mask[:], mask_s)])

        def windowed(after):
            layernorm(X, Z, ahead=windowed_loads(0))
            for l in range(DEPTH):
                windowed_prep(l)
                attention(1, True, True, Z)
                arrive()
                shift_tokens()
                layernorm(H, H, ahead=windowed_loads(l + 1) if l + 1 < DEPTH else after)
                feed_forward()
            axpy_half()

        def sliding():
            layernorm(X, Z, rms=True)
            arrive()
            attention(2, False, False, X)

        windowed(sliding_loads())
        if STAGES >= 2:
            sliding()
        if STAGES >= 3:
            windowed(())
        FX.close()
        GX = ExitStack()

        def gb(name, shape, dt=F32):
            return GX.enter_context(nc.sbuf_tensor(name, shape, dt))

        LW = gb("LW", [P, 3 * C])
        LWO = gb("LWO", [P, C])
        lmin = gb("lmin", [P, 3 * C])
        lexp = gb("lexp", [P, 3 * C])
        lqk = gb("lqk", [P, 2, 3 * C])
        lqm = gb("lqm", [P, LH, P])
        lv = gb("lv", [P, 2, C])
        lvp = gb("lvp", [P, 2, 4 * (P + LD)])
        att = gb("att", [P, LH, P])
        state = gb("state", [P, C])
        suse = gb("suse", [P, C])
        sadd = gb("sadd", [P, C])
        den = gb("den", [P, P])
        rden = gb("rden", [P, P])
        prod = gb("prod", [P, P])
        ksum = gb("ksum", [P, 1])
        kuse = gb("kuse", [P, 1])
        loT = gb("loT", [P, P])
        rowm = gb("rowm", [P, LH])
        trilm = gb("trilm", [P, P])
        blkm = gb("blkm", [P, C])
        E1 = gb("E1", [P, EX, EH])
        E3 = gb("E3", [P, EX, EH])
        E2 = gb("E2", [P, EX, 2, C])
        wgT = gb("wgT", [P, EX])
        trib = gb("trib", [P, P], BF16)
        onesb = gb("onesb", [P, P], BF16)
        onesf = gb("onesf", [P, P])
        zerob = gb("zerob", [P, P], BF16)
        iotab = gb("iotab", [P, P], BF16)
        iota4f = gb("iota4f", [P, SG])
        tokh = gb("tokh", [P, NT * EX])
        tokl = gb("tokl", [P, NT * EX])
        scm = gb("scm", [P, EX * NT])

        def late_loads():
            return ([(LW[:], lwqkv), (LWO[:], lwo), (rowm[:], rowmask), (trilm[:], tril), (blkm[:], blockm),
                   (E1[:], ew1.rearrange("e c h -> c e h")), (E3[:], ew3.rearrange("e c h -> c e h")),
                   (E2[:], ew2.rearrange("e (a p) c -> p e a c", p=P)), (wgT[:], wg), (trib[:], tri),
                   (onesb[:], ones), (iotab[:], iota), (iota4f[:], iota4), (tokh[:], tokhi), (tokl[:], toklo),
                   (scm[:], scanm)])

        def late_init():
            with nc.Block() as block:
                @block.vector
                def _(dve):
                    dve.memset(onesf[:], 1.0)
                    dve.memset(zerob[:], 0.0)
                    dve.memset(lvp[:], 0.0)
                    dve.memset(ksum[:], 0.0)
                    dve.memset(state[:], 0.0)

        def linear():
            L = {k: sem("l_" + k) for k in ("ybuf", "t", "hT", "qkv", "min", "v", "vp", "exp", "qk", "qm", "at", "att",
                                            "kuse", "suse", "kc", "prod", "norm", "den", "rden", "o", "u", "sadd",
                                            "state", "on", "y", "res")}
            psA = [psF[:, 1, :], psF[:, 2, :], psS[:, 0, :], psS[:, 1, :]]

            def early(m, k):
                return isinstance(m.count, int) and m.count < k

            with nc.Block() as block:
                @block.tensor
                def _(pe):
                    def values(m, r, heads):
                        for i in heads:
                            last = nc.tensor.matmul(psO[32 * r:32 * r + 32, 0:P], lvp[:, m.parity, P * i + 32 * r:P * i + 32 * r + 32],
                                                    att[:, 4 * r + i, :], start=False, stop=(i == 3),
                                                    skip_group_check=True, tile_position=(0, 32 * r))
                        return last

                    def step(e, f, n, m):
                        if f is not None:
                            pe.wait_ge(L["ybuf"], f.done())
                            if m is not None and not early(m, 1):
                                pe.wait_ge(L["sadd"], m.done(1))
                            elif n is not None:
                                pe.wait_ge(L["hT"], n.done())
                            nc.tensor.transpose(psP[:, 1, 0:P], ybuf[:, 0, 0:P], idt[:]).then_inc(L["t"], 1)
                        if m is not None:
                            if not early(m, 1):
                                pe.wait_ge(L["den"], m.done(1))
                            nc.tensor.matmul(psP[:, 0, 0:P], lqk[:, m.parity, 2 * C:3 * C], trilm[:],
                                             start=True, stop=True).then_inc(L["kc"], 1)
                            pe.wait_ge(L["suse"], m.done())
                            if not early(m, 1):
                                pe.wait_ge(L["res"], m.done(1))
                            nc.tensor.matmul(psO[:, 0:P], suse[:], lqk[:, m.parity, 0:P], start=True, stop=False,
                                             skip_group_check=True)
                            pe.wait_ge(L["vp"], m.done())
                            for r in range(4):
                                pe.wait_ge(L["att"], 4 * m.count + r + 1)
                                last = values(m, r, range(4))
                                if r == 1:
                                    pe.wait_ge(L["prod"], m.done())
                                    nc.tensor.matmul(psP[:, 0, P:2 * P], blkm[:], prod[:], start=True,
                                                     stop=True).then_inc(L["norm"], 1)
                            last.then_inc(L["o"], 1)
                            if f is not None:
                                pe.wait_ge(L["hT"], f.done())
                            elif not early(m, 1):
                                pe.wait_ge(L["sadd"], m.done(1))
                            nc.tensor.matmul(psP[:, 1, 0:P], lqk[:, m.parity, 2 * C:3 * C],
                                             lv[:, m.parity, :], start=True, stop=True).then_inc(L["u"], 1)
                        if f is not None:
                            pe.wait_ge(L["hT"], f.done())
                            if n is not None:
                                pe.wait_ge(L["qk"], n.done())
                            for a in range(2):
                                nc.tensor.matmul(psF[:, 0, a * P:(a + 1) * P], LW[:, a * C:(a + 1) * C], hT[:, 0, 0:P],
                                                 start=True, stop=True)
                            nc.tensor.matmul(psF[:, 0, 2 * P:4 * P], hT[:, 0, 0:P], LW[:, C:3 * C], start=True,
                                             stop=True).then_inc(L["qkv"], 1)
                        for r in range(4):
                            if n is not None:
                                pe.wait_ge(L["qm"], 4 * n.count + r + 1)
                                nc.tensor.matmul(psA[r], lqk[:, n.parity, P:2 * P], lqm[:, 4 * r:4 * r + 4, :],
                                                 start=True, stop=True).then_inc(L["at"], 1)
                            if r == 1 and m is not None:
                                pe.wait_ge(L["on"], m.done())
                                nc.tensor.matmul(psO[:, P:P + C], loT[:], LWO[:], start=True, stop=True).then_inc(L["y"], 1)
                    pipeline(pe, 1, NT, 0, step, stages=4)

                @block.scalar
                def _(act):
                    act.preload_act_table_set("natural_log_exp_and_others")

                    def step(e, f, n, m):
                        if f is not None:
                            act.wait_ge(L["t"], f.done())
                            if n is not None:
                                act.wait_ge(L["qkv"], n.done())
                            nc.scalar.copy(hT[:, 0, 0:P], psP[:, 1, 0:P]).then_inc(L["hT"], 1)
                            act.wait_ge(L["min"], f.done())
                            if m is not None:
                                act.wait_ge(L["u"], m.done())
                            nc.scalar.copy(lv[:, f.parity, :], psF[:, 0, 3 * C:4 * C]).then_inc(L["v"], 1)
                            if n is not None:
                                act.wait_ge(L["qk"], n.done())
                            nc.scalar.activation(lexp[:], lmin[:], ACT.Exp).then_inc(L["exp"], 1)
                            act.wait_ge(L["v"], f.done())
                            nc.scalar.copy(lvp[:, f.parity, :].rearrange("p (i c) -> p i c", i=4)[:, :, 0:P]
                                           .rearrange("p i (r c) -> p i r c", r=4)[:, :, :, 0:LD],
                                           lv[:, f.parity, :].rearrange("p (r i d) -> p i r d", r=4, i=4)).then_inc(L["vp"], 1)
                    pipeline(act, 1, NT, 0, step, stages=4)

                @block.gpsimd
                def _(pool):
                    def step(e, f, n, m):
                        if n is not None:
                            pool.wait_ge(L["qk"], n.done())
                            for r in range(4):
                                if m is not None:
                                    pool.wait_ge(L["at"], 4 * m.count + r + 1)
                                nc.gpsimd.tensor_tensor(lqm[:, 4 * r:4 * r + 4, :],
                                                        lqk[:, n.parity, 0:P].unsqueeze(1).to_broadcast([P, 4, P]),
                                                        rowm[:, 4 * r:4 * r + 4].unsqueeze(2).to_broadcast([P, 4, P]),
                                                        ALU.mult).then_inc(L["qm"], 1)
                    pipeline(pool, 1, NT, 0, step, stages=4)

                @block.vector
                def _(dve):
                    def step(e, f, n, m):
                        if e is not None:
                            if f is not None:
                                dve.wait_ge(L["t"], f.done())
                            nc.vector.tensor_scalar(ybuf[:, 0, 0:P], Z[:, e.tile, :], 1.0, None, ALU.mult).then_inc(L["ybuf"], 1)
                        if m is not None:
                            dve.wait_ge(L["kc"], m.done())
                            dve.wait_ge(L["kuse"], m.done())
                            nc.vector.scalar_tensor_tensor(prod[:], psP[:, 0, 0:P], kuse[:], lqk[:, m.parity, 0:P],
                                                           ALU.add, ALU.mult)
                            nc.vector.tensor_tensor(ksum[:], psP[:, 0, P - 1:P], kuse[:], ALU.add).then_inc(L["prod"], 1)
                            dve.wait_ge(L["norm"], m.done())
                            nc.vector.tensor_scalar(den[:], psP[:, 0, P:2 * P], 1e-6, None, ALU.max).then_inc(L["den"], 1)
                            dve.wait_ge(L["den"], m.done())
                            nc.vector.reciprocal(rden[:], den[:]).then_inc(L["rden"], 1)
                            dve.wait_ge(L["rden"], m.done())
                            dve.wait_ge(L["o"], m.done())
                            if not early(m, 1):
                                dve.wait_ge(L["y"], m.done(1))
                            nc.vector.tensor_tensor(loT[:], psO[:, 0:P], rden[:], ALU.mult).then_inc(L["on"], 1)
                            dve.wait_ge(L["u"], m.done())
                            nc.vector.tensor_tensor(sadd[:], psP[:, 1, 0:P], blkm[:], ALU.mult).then_inc(L["sadd"], 1)
                            dve.wait_ge(L["sadd"], m.done())
                            nc.vector.tensor_tensor(state[:], suse[:], sadd[:], ALU.add).then_inc(L["state"], 1)
                            dve.wait_ge(L["state"], m.done())
                        if n is not None:
                            nc.vector.tensor_scalar(kuse[:], ksum[:], keep_sb[:, bass.ds(n.tile, 1)], None,
                                                    ALU.mult).then_inc(L["kuse"], 1)
                            nc.vector.tensor_scalar(suse[:], state[:], keep_sb[:, bass.ds(n.tile, 1)], None,
                                                    ALU.mult).then_inc(L["suse"], 1)
                        if f is not None:
                            dve.wait_ge(L["qkv"], f.done())
                            if n is not None:
                                dve.wait_ge(L["exp"], n.done())
                            nc.vector.tensor_scalar(lmin[:], psF[:, 0, 0:3 * C], 0.0, None, ALU.min).then_inc(L["min"], 1)
                        for r in range(4):
                            if n is not None:
                                dve.wait_ge(L["at"], 4 * n.count + r + 1)
                                nc.vector.tensor_tensor(att[:, 4 * r:4 * r + 4, :],
                                                        psA[r].rearrange("p (h n) -> p h n", n=P),
                                                        trilm[:].unsqueeze(1).to_broadcast([P, 4, P]),
                                                        ALU.mult).then_inc(L["att"], 1)
                            if r == 0 and f is not None:
                                dve.wait_ge(L["exp"], f.done())
                                nc.vector.scalar_tensor_tensor(lqk[:, f.parity, :], psF[:, 0, 0:3 * C], 0.0, lexp[:],
                                                               ALU.max, ALU.add).then_inc(L["qk"], 1)
                            if r == 2 and m is not None:
                                dve.wait_ge(L["y"], m.done())
                                nc.vector.tensor_tensor(X[:, m.tile, :], X[:, m.tile, :], psO[:, P:P + C],
                                                        ALU.add).then_inc(L["res"], 1)
                    pipeline(dve, 1, NT, 0, step, stages=4)

        NE = NT * EX
        SC = gb("SC", [P, NT, EX])
        gt = gb("gt", [P, 2, 4 * P])
        y4 = gb("y4", [P, 2, 4 * P])
        ext = gb("ext", [P, 2 * EX])
        gext = gb("gext", [P, 2 * EX])
        lo_t = gb("lo_t", [P, EX])
        hi_t = gb("hi_t", [P, EX])
        mid = gb("mid", [P, 3, EX])
        both = gb("both", [P, 2, 3, EX])
        big = gb("big", [P, 3, EX])
        best = gb("best", [P, 2, EX])
        tot3 = gb("tot3", [P, 3, EX])
        tot = gb("tot", [P, EX])
        need = gb("need", [P, EX])
        ge = gb("ge", [P, NT, EX], BF16)
        ge3 = gb("ge3", [P, 3, NT, EX], BF16)
        selh = gb("selh", [P, NT, EX], BF16)
        tie = gb("tie", [P, NT, EX], BF16)
        sel = gb("sel", [P, NT, EX], BF16)
        totT = gb("totT", [P, EX, NT])
        inc = gb("inc", [P, EX, NT])
        pos = gb("pos", [P, NT, EX])
        bsl = gb("bsl", [P, NT, EX])
        tmp3 = gb("tmp3", [P, NT, EX])
        B4 = gb("B4", [P, NE, SG])
        R = gb("R", [P, NE, 5, SG], BF16)
        s1 = gb("s1", [P, NE], BF16)
        s2 = gb("s2", [P, NE], BF16)
        s3 = gb("s3", [P, NE], BF16)
        hot = gb("hot", [P, 2, EX, P], BF16)
        G = gb("G", [P, EX, 5, SG])
        idx = gb("idx", [P, EX, SG], U32)
        ssl = gb("ssl", [P, EX, SG])
        esl = gb("esl", [P, EX, SG])
        wsl = gb("wsl", [P, EX, SG])
        esum = gb("esum", [P, EX])
        xg = gb("xg", [P, AHEAD, SG, C])
        xgT = gb("xgT", [P, 2, CAP])
        sil = gb("sil", [P, 2, CAP])
        hE = gb("hE", [P, 2, 2, CAP])
        ysb = gb("ysb", [P, 2, SG, C])
        yd = nc.dram_tensor("yd", (BATCH * SEQ, C), F32).ap()
        acc = nc.dram_tensor("acc", (BATCH * SEQ, C), F32).ap()
        gathered = [sem(f"gathered{u}") for u in range(AHEAD)]
        scattered = sem("scattered")
        chain = sem("chain")
        n_chain = [0]
        M = {k: sem("m_" + k) for k in ("lo", "hi", "ybuf", "t", "gT", "g", "sc", "ext", "all", "cmp", "cnt", "step", "pre", "hot",
                                        "comp", "clear", "ex", "sum", "et", "eT", "up", "sil", "h", "down", "ysb")}
        n_m = {k: 0 for k in ("mix", "gate", "search", "pre", "hot", "ex", "ssum")}

        def link(dve, ins):
            n_chain[0] += 1
            ins.then_inc(chain, 1)
            dve.wait_ge(chain, n_chain[0])

        def gate(target):
            base = n_m["gate"]
            rounds = NT // 4
            n_m["gate"] += rounds

            with nc.Block() as block:
                @block.sync
                def _(sp):
                    sp.dma_start(yd.rearrange("(t p) c -> p t c", p=P), Z[:]).then_inc(stored, 16)
                    sp.dma_start(target.rearrange("(t p) c -> p t c", p=P), X[:]).then_inc(stored, 16)
                    n_store[0] += 32

                @block.vector
                def _(dve):
                    def step(n, m, k):
                        if n is not None:
                            if k is not None:
                                dve.wait_ge(M["t"], k.done())
                            nc.vector.tensor_scalar(y4[:, n.parity].rearrange("p (t c) -> p t c", c=C),
                                                    Z[:, bass.ds(4 * n.tile, 4), :], 1.0, None, ALU.mult).then_inc(M["ybuf"], 1)
                        if m is not None:
                            dve.wait_ge(M["g"], m.done())
                            nc.vector.tensor_scalar(SC[:, bass.ds(4 * m.tile, 4), :],
                                                    psP[:, m.parity, 0:4 * EX].rearrange("p (t e) -> p t e", e=EX),
                                                    1.0, None, ALU.mult).then_inc(M["sc"], 1)
                    pipeline(dve, 1, rounds, base, step)

                @block.tensor
                def _(pe):
                    def step(n, m, k):
                        if n is not None:
                            pe.wait_ge(M["ybuf"], n.done())
                            if k is not None:
                                pe.wait_ge(M["gT"], k.done())
                            for j in range(4):
                                last = nc.tensor.transpose(psS[:, n.parity, j * P:(j + 1) * P], y4[:, n.parity, j * P:(j + 1) * P],
                                                           idt[:])
                            last.then_inc(M["t"], 1)
                        if m is not None:
                            pe.wait_ge(M["gT"], m.done())
                            if k is not None:
                                pe.wait_ge(M["sc"], k.done())
                            for j in range(4):
                                last = nc.tensor.matmul(psP[:, m.parity, j * EX:(j + 1) * EX], gt[:, m.parity, j * P:(j + 1) * P],
                                                        wgT[:], start=True, stop=True)
                            last.then_inc(M["g"], 1)
                    pipeline(pe, 1, rounds, base, step)

                @block.scalar
                def _(act):
                    def step(n, m, k):
                        if n is not None:
                            act.wait_ge(M["t"], n.done())
                            if k is not None:
                                act.wait_ge(M["g"], k.done())
                            nc.scalar.copy(gt[:, n.parity, :], psS[:, n.parity, :]).then_inc(M["gT"], 1)
                    pipeline(act, 1, rounds, base, step)

        def search():
            base = n_m["search"]
            n_m["search"] += SEARCH
            m0 = n_m["mix"]
            BIG = 1e37
            with nc.Block() as block:
                @block.vector
                def _(dve):
                    se = SC[:].rearrange("p t e -> p e t")
                    counts = psS[:, :, :].rearrange("p b n -> p (b n)")[:, 0:3 * NE].rearrange("p (j t e) -> p j e t", j=3, e=EX)
                    nc.vector.tensor_reduce(ext[:, 0:EX], se, AX.X, ALU.max)
                    nc.vector.tensor_reduce(ext[:, EX:2 * EX], se, AX.X, ALU.min, negate=True).then_inc(M["ext"], 1)
                    dve.wait_ge(M["all"], m0 + 1)
                    nc.vector.tensor_scalar(lo_t[:], gext[:, EX:2 * EX], -1.0, None, ALU.mult)
                    link(dve, nc.vector.tensor_tensor(hi_t[:], gext[:, 0:EX], gext[:, EX:2 * EX], ALU.max))
                    link(dve, nc.vector.tensor_scalar(hi_t[:], hi_t[:], 2.0 ** -10, 1e-30, ALU.mult, ALU.add))
                    link(dve, nc.vector.tensor_tensor(hi_t[:], hi_t[:], gext[:, 0:EX], ALU.add))

                    K = 9
                    sbase = base * K

                    def body(i):
                        at = [0]

                        def also(ins):
                            at[0] += 1
                            ins.then_inc(M["step"], 1)

                        def nxt(ins):
                            also(ins)
                            dve.wait_ge(M["step"], i * K + (sbase + at[0]))

                        nxt(nc.vector.tensor_tensor(mid[:, 0], lo_t[:], hi_t[:], ALU.add))
                        nxt(nc.vector.tensor_scalar(mid[:, 0], mid[:, 0], 0.5, None, ALU.mult))
                        also(nc.vector.tensor_tensor(mid[:, 1], lo_t[:], mid[:, 0], ALU.add))
                        nxt(nc.vector.tensor_tensor(mid[:, 2], hi_t[:], mid[:, 0], ALU.add))
                        nxt(nc.vector.tensor_scalar(mid[:, 1:3], mid[:, 1:3], 0.5, None, ALU.mult))
                        for j in range(3):
                            nc.vector.tensor_tensor(ge3[:, j], SC[:], mid[:, j].unsqueeze(1).to_broadcast([P, NT, EX]),
                                                    ALU.is_ge).then_inc(M["cmp"], 1)
                        dve.wait_ge(M["cnt"], i + (base + 1))
                        nxt(nc.vector.tensor_reduce(tot3[:], counts, AX.X, ALU.add))
                        nxt(nc.vector.tensor_scalar(big[:], tot3[:], CAP - 0.5, BIG, ALU.is_ge, ALU.mult))
                        also(nc.vector.scalar_tensor_tensor(both[:, 0, 0:3], big[:], -BIG, mid[:], ALU.add, ALU.add))
                        nxt(nc.vector.tensor_tensor(both[:, 1, 0:3], big[:], mid[:], ALU.add))
                        assert at[0] == K
                        nc.vector.tensor_reduce(best[:, 0], both[:, 0].rearrange("p j e -> p e j"), AX.X,
                                                ALU.max).then_inc(M["lo"], 1)
                        nc.vector.tensor_reduce(best[:, 1], both[:, 1].rearrange("p j e -> p e j"), AX.X,
                                                ALU.min).then_inc(M["hi"], 1)
                        dve.wait_ge(M["lo"], 2 * i + (2 * base + 1))
                        dve.wait_ge(M["hi"], 2 * i + (2 * base + 1))
                        nc.vector.tensor_tensor(lo_t[:], lo_t[:], best[:, 0], ALU.max).then_inc(M["lo"], 1)
                        nc.vector.tensor_tensor(hi_t[:], hi_t[:], best[:, 1], ALU.min).then_inc(M["hi"], 1)
                        dve.wait_ge(M["lo"], 2 * i + (2 * base + 2))
                        dve.wait_ge(M["hi"], 2 * i + (2 * base + 2))

                    body(0)
                    with dve.Fori(1, SEARCH, 4) as i:
                        for u in range(4):
                            body(i + u)

                @block.gpsimd
                def _(pool):
                    pool.wait_ge(M["ext"], m0 + 1)
                    nc.gpsimd.partition_all_reduce(gext[:], ext[:], P, RMAX).then_inc(M["all"], 1)

                @block.tensor
                def _(pe):
                    def body(i):
                        for j in range(3):
                            pe.wait_ge(M["cmp"], 3 * i + (3 * base + 2 * m0 + j + 1))
                            last = nc.tensor.matmul(psS[:, j // 2, (j % 2) * NE:(j % 2 + 1) * NE], onesb[:],
                                                    ge3[:, j].rearrange("p t e -> p (t e)"), start=True, stop=True)
                        last.then_inc(M["cnt"], 1)
                    body(0)
                    with pe.Fori(1, SEARCH, 4) as i:
                        for u in range(4):
                            body(i + u)

        def choose():
            p0 = n_m["pre"]
            n_m["pre"] += 3
            te = "p t e -> p (t e)"
            with nc.Block() as block:
                @block.vector
                def _(dve):
                    bc = lambda a: a[:].unsqueeze(1).to_broadcast([P, NT, EX])

                    def prefix(v, which):
                        dve.wait_ge(M["pre"], p0 + which)
                        link(dve, nc.vector.tensor_copy(totT[:], psS[:, 1, 0:NE].rearrange("p (t e) -> p e t", e=EX)))
                        link(dve, nc.vector.tensor_tensor_scan(inc[:].rearrange("p e t -> p (e t)"), scm[:],
                                                               totT[:].rearrange("p e t -> p (e t)"), 0.0, ALU.mult, ALU.add))
                        link(dve, nc.vector.tensor_tensor(inc[:], inc[:], totT[:], ALU.subtract))
                        link(dve, nc.vector.tensor_tensor(pos[:], psS[:, 0, 0:NE].rearrange("p (t e) -> p t e", e=EX),
                                                          inc[:].rearrange("p e t -> p t e"), ALU.add))

                    nc.vector.tensor_tensor(ge[:], SC[:], bc(lo_t), ALU.is_ge)
                    link(dve, nc.vector.tensor_tensor(selh[:], SC[:], bc(hi_t), ALU.is_ge))
                    nc.vector.tensor_tensor(tie[:], ge[:], selh[:], ALU.subtract).then_inc(M["cmp"], 1)
                    sf = SC[:].rearrange(te)
                    link(dve, nc.vector.tensor_copy(s1[:], sf))
                    link(dve, nc.vector.tensor_tensor(tmp3[:].rearrange(te), sf, s1[:], ALU.subtract))
                    link(dve, nc.vector.tensor_copy(s2[:], tmp3[:].rearrange(te)))
                    link(dve, nc.vector.tensor_tensor(s3[:], tmp3[:].rearrange(te), s2[:], ALU.subtract))
                    dve.wait_ge(M["pre"], p0 + 1)
                    link(dve, nc.vector.tensor_reduce(tot[:], psO[:, 0:NE].rearrange("p (t e) -> p e t", e=EX), AX.X, ALU.add))
                    link(dve, nc.vector.tensor_scalar(need[:], tot[:], -1.0, float(CAP), ALU.mult, ALU.add))
                    prefix(tie, 2)
                    link(dve, nc.vector.tensor_tensor(tmp3[:], pos[:], bc(need), ALU.is_lt))
                    link(dve, nc.vector.tensor_tensor(tmp3[:], tmp3[:], tie[:], ALU.mult))
                    link(dve, nc.vector.tensor_tensor(sel[:], tmp3[:], selh[:], ALU.add))
                    nc.vector.tensor_scalar(tmp3[:], sel[:], -4096.0, 4096.0, ALU.mult, ALU.add).then_inc(M["cmp"], 1)
                    prefix(sel, 3)
                    link(dve, nc.vector.tensor_tensor(pos[:], pos[:], tmp3[:], ALU.add))
                    link(dve, nc.vector.tensor_scalar(bsl[:], pos[:], float(P), None, ALU.is_ge))
                    for b in range(2, SG):
                        link(dve, nc.vector.scalar_tensor_tensor(bsl[:], pos[:], float(b * P), bsl[:], ALU.is_ge, ALU.add))
                    link(dve, nc.vector.scalar_tensor_tensor(pos[:], bsl[:], -float(P), pos[:], ALU.mult, ALU.add))
                    link(dve, nc.vector.tensor_tensor(B4[:], bsl[:].rearrange(te).unsqueeze(2).to_broadcast([P, NE, SG]),
                                                      iota4f[:].unsqueeze(1).to_broadcast([P, NE, SG]), ALU.is_equal))
                    for v, val in enumerate((tokh, tokl, s1, s2, s3)):
                        nc.vector.tensor_tensor(R[:, :, v, :], B4[:], val[:].unsqueeze(2).to_broadcast([P, NE, SG]), ALU.mult)

                @block.tensor
                def _(pe):
                    c0 = n_cmp()
                    pe.wait_ge(M["cmp"], c0 + 1)
                    nc.tensor.matmul(psO[:, 0:NE], onesb[:], selh[:].rearrange(te), start=True, stop=True).then_inc(M["pre"], 1)
                    nc.tensor.matmul(psS[:, 0, 0:NE], trib[:], tie[:].rearrange(te), start=True, stop=True)
                    nc.tensor.matmul(psS[:, 1, 0:NE], onesb[:], tie[:].rearrange(te), start=True, stop=True).then_inc(M["pre"], 1)
                    pe.wait_ge(M["cmp"], c0 + 2)
                    nc.tensor.matmul(psS[:, 0, 0:NE], trib[:], sel[:].rearrange(te), start=True, stop=True)
                    nc.tensor.matmul(psS[:, 1, 0:NE], onesb[:], sel[:].rearrange(te), start=True, stop=True).then_inc(M["pre"], 1)

        def n_cmp():
            return 3 * n_m["search"] + 2 * n_m["mix"]

        def compact():
            base = n_m["hot"]
            n_m["hot"] += NT
            m0 = n_m["mix"]
            with nc.Block() as block:
                @block.vector
                def _(dve):
                    def body(T, u):
                        if isinstance(T, int) and T + u < 2:
                            pass
                        else:
                            dve.wait_ge(M["comp"], base + T + u - 1)
                        nc.vector.tensor_tensor(hot[:, u], iotab[:].unsqueeze(1).to_broadcast([P, EX, P]),
                                                pos[:, T + u, :].unsqueeze(2).to_broadcast([P, EX, P]),
                                                ALU.is_equal).then_inc(M["hot"], 1)
                    body(0, 0)
                    body(0, 1)
                    with dve.Fori(2, NT, 2) as T:
                        T = T.with_bounds(min_val=2, max_val=NT - 2)
                        for u in range(2):
                            body(T, u)

                @block.tensor
                def _(pe):
                    def body(T, u):
                        pe.wait_ge(M["hot"], base + T + u + 1)
                        for e in range(EX):
                            last = nc.tensor.matmul(psO[:, 20 * e:20 * e + 20], hot[:, u, e, :],
                                                    R[:, EX * T + (EX * u + e)].rearrange("p v b -> p (v b)"),
                                                    start=False, stop=False, skip_group_check=True)
                        last.then_inc(M["comp"], 1)
                    nc.tensor.matmul(psO[:, 0:20 * EX], zerob[:], R[:, 0:EX].rearrange("p t v b -> p (t v b)"),
                                     start=True, stop=False, skip_group_check=True)
                    body(0, 0)
                    body(0, 1)
                    with pe.Fori(2, NT, 2) as T:
                        T = T.with_bounds(min_val=2, max_val=NT - 2)
                        for u in range(2):
                            body(T, u)

            with nc.Block() as block:
                @block.vector
                def _(dve):
                    link(dve, nc.vector.tensor_copy(G[:], psO[:, 0:20 * EX].rearrange("p (e v b) -> p e v b", e=EX, v=5)))
                    nc.vector.scalar_tensor_tensor(idx[:], G[:, :, 0, :], float(P), G[:, :, 1, :], ALU.mult, ALU.add)
                    link(dve, nc.vector.tensor_tensor(ssl[:], G[:, :, 2, :], G[:, :, 3, :], ALU.add))
                    link(dve, nc.vector.tensor_tensor(ssl[:], ssl[:], G[:, :, 4, :], ALU.add))
                    nc.vector.tensor_tensor(ssl[:], ssl[:], gext[:, 0:EX].unsqueeze(2).to_broadcast([P, EX, SG]),
                                            ALU.subtract).then_inc(M["ex"], 1)
                    dve.wait_ge(M["ex"], 2 * m0 + 2)
                    nc.vector.tensor_reduce(esum[:], esl[:], AX.X, ALU.add).then_inc(M["sum"], 1)
                    dve.wait_ge(M["sum"], 2 * m0 + 2)
                    link(dve, nc.vector.reciprocal(tot[:], psS[:, 0, 0:EX]))
                    nc.vector.scalar_tensor_tensor(wsl[:], esl[:], 0.5, tot[:].unsqueeze(2).to_broadcast([P, EX, SG]),
                                                   ALU.mult, ALU.mult)

                @block.scalar
                def _(act):
                    act.wait_ge(M["ex"], 2 * m0 + 1)
                    nc.scalar.activation(esl[:], ssl[:], ACT.Exp).then_inc(M["ex"], 1)

                @block.tensor
                def _(pe):
                    pe.wait_ge(M["sum"], 2 * m0 + 1)
                    nc.tensor.matmul(psS[:, 0, 0:EX], onesf[:], esum[:], start=True, stop=True).then_inc(M["sum"], 1)

        def experts(target):
            m0 = n_m["mix"]
            b = EX * m0
            with nc.Block() as block:
                @block.gpsimd
                def _(pool):
                    def gather(e):
                        if e >= AHEAD:
                            pool.wait_ge(M["et"], b + e - AHEAD + 1)
                        for g in range(SG):
                            pool.indirect_dma_start(out=xg[:, e % AHEAD, g, :], out_offset=None, in_=yd[:, :],
                                                    in_offset=bass.IndirectOffsetOnAxis(ap=idx[:, e, g:g + 1], axis=0)
                                                    ).then_inc(gathered[e % AHEAD], 16)

                    def scatter(e):
                        pool.wait_ge(M["ysb"], b + e + 1)
                        if b + e > 0:
                            pool.wait_ge(scattered, 16 * SG * (b + e))
                        for g in range(SG):
                            pool.indirect_dma_start(out=target[:, :],
                                                    out_offset=bass.IndirectOffsetOnAxis(ap=idx[:, e, g:g + 1], axis=0),
                                                    in_=ysb[:, e % 2, g, :], in_offset=None,
                                                    compute_op=ALU.add).then_inc(scattered, 16)

                    for e in range(AHEAD - 1):
                        gather(e)
                    for e in range(EX):
                        scatter(e)
                        if e + AHEAD - 1 < EX:
                            gather(e + AHEAD - 1)
                    pool.wait_ge(scattered, 16 * SG * (b + EX))

                @block.tensor
                def _(pe):
                    def turn(e):
                        pe.wait_ge(gathered[e % AHEAD], 16 * SG * ((b + e) // AHEAD + 1))
                        if b + e > 0:
                            pe.wait_ge(M["eT"], b + e)
                        for g in range(SG):
                            last = nc.tensor.transpose(psP[:, 0, g * P:(g + 1) * P], xg[:, e % AHEAD, g, :], idt[:])
                        last.then_inc(M["et"], 1)

                    def up(e):
                        pe.wait_ge(M["eT"], b + e + 1)
                        for c in range(2):
                            if 2 * (b + e) + c >= 2:
                                pe.wait_ge(M["h"], 2 * (b + e) + c - 1)
                            nc.tensor.matmul(psS[:, c, :], E1[:, e, c * P:(c + 1) * P], xgT[:, e % 2, :], start=True, stop=True)
                            nc.tensor.matmul(psF[:, c, :], E3[:, e, c * P:(c + 1) * P], xgT[:, e % 2, :], start=True,
                                             stop=True).then_inc(M["up"], 1)

                    def down(e):
                        pe.wait_ge(M["h"], 2 * (b + e) + 2)
                        if b + e > 0:
                            pe.wait_ge(M["ysb"], b + e)
                        for g in range(SG):
                            for c in range(2):
                                last = nc.tensor.matmul(psO[:, g * C:(g + 1) * C], hE[:, e % 2, c, g * P:(g + 1) * P],
                                                        E2[:, e, c, :], start=(c == 0), stop=(c == 1))
                        last.then_inc(M["down"], 1)

                    for e in range(EX):
                        turn(e)
                        up(e)
                        down(e)

                @block.scalar
                def _(act):
                    def turned(e):
                        act.wait_ge(M["et"], b + e + 1)
                        if b + e >= 2:
                            act.wait_ge(M["up"], 2 * (b + e) - 2)
                        nc.scalar.copy(xgT[:, e % 2, :], psP[:, 0, :]).then_inc(M["eT"], 1)

                    turned(0)
                    for e in range(EX):
                        for c in range(2):
                            act.wait_ge(M["up"], 2 * (b + e) + c + 1)
                            if b + e > 0:
                                act.wait_ge(M["h"], 2 * (b + e) + c - 1)
                            nc.scalar.activation(sil[:, c, :], psS[:, c, :], ACT.Silu).then_inc(M["sil"], 1)
                        if e + 1 < EX:
                            turned(e + 1)

                @block.vector
                def _(dve):
                    def out_rows(e):
                        dve.wait_ge(M["down"], b + e + 1)
                        if b + e >= 2:
                            dve.wait_ge(scattered, 16 * SG * (b + e - 1))
                        nc.vector.tensor_tensor(ysb[:, e % 2], psO[:, :].rearrange("p (g c) -> p g c", c=C),
                                                wsl[:, e, :].unsqueeze(2).to_broadcast([P, SG, C]),
                                                ALU.mult).then_inc(M["ysb"], 1)

                    for e in range(EX):
                        for c in range(2):
                            dve.wait_ge(M["sil"], 2 * (b + e) + c + 1)
                            if b + e >= 2:
                                dve.wait_ge(M["down"], b + e - 1)
                            nc.vector.tensor_tensor(hE[:, e % 2, c, :], sil[:, c, :], psF[:, c, :], ALU.mult).then_inc(M["h"], 1)
                        out_rows(e)

        def mixture(target, ahead=()):
            layernorm(X, Z, ahead=ahead)
            arrive()
            gate(target)
            search()
            choose()
            compact()
            with nc.Block() as block:
                @block.sync
                def _(sp):
                    sp.wait_ge(stored, n_store[0])
            experts(target)
            n_m["mix"] += 1

        if STAGES >= 4:
            late_init()
            mixture(acc if STAGES > 4 else out, late_loads())
        if STAGES >= 5:
            start_loads([(X[:], acc.rearrange("(t p) c -> p t c", p=P))])
            arrive()
            layernorm(X, Z)
            linear()
        if STAGES >= 6:
            mixture(out)
        if STAGES not in (4, 6):
            with nc.Block() as block:
                @block.sync
                def _(sp):
                    n_store[0] += 16
                    sp.dma_start(out.rearrange("(t p) c -> p t c", p=P), X[:]).then_inc(stored, 16)
                    sp.wait_ge(stored, n_store[0])
        GX.close()


def constants():
    import numpy as np

    f = np.float32

    def bf16_bits(a):
        return (np.ascontiguousarray(a, f).view(np.uint32) >> 16).astype(np.uint16)

    half = np.arange(0, HD, 2, dtype=f)
    inv = (f(1.0) / np.power(f(10000.0), half / f(HD))).astype(f)
    t = np.arange(SEQ, dtype=f)
    fr = (t[:, None] * inv[None, :]).astype(f)
    fr = np.concatenate([fr, fr], -1)
    cos, sin = np.cos(fr).astype(f), np.sin(fr).astype(f)
    sign = np.concatenate([-np.ones(HD // 2), np.ones(HD // 2)]).astype(f)
    basis = (half + f(0.4 * HD)) / f(1.4 * HD)
    power = (t - SEQ // 2) / f(32.0)
    sc = np.power(basis[None, :], power[:, None]).astype(f)
    sc = np.concatenate([sc, sc], -1)

    def pack(cq, sq_, ck, sk):
        a = np.stack([np.stack([cq, ck], 1), np.stack([sq_, sk], 1)], 1)
        return np.ascontiguousarray(a.reshape(TPB, P, 2, 2, HD).transpose(1, 0, 2, 3, 4)).astype(f)

    c = {}
    c["rope_a"] = pack(8 * cos * sc, 8 * sin * sc * sign, cos / sc, sin / sc * sign)
    c["rope_b"] = np.zeros((1, 1), f)
    c["arope"] = pack(cos / 8, sin * sign / 8, cos, sin * sign)

    def band(look):
        i = (np.arange(P)[:, None] % BQ) + BQ
        j = np.arange(P)[None, :]
        m = np.where((j <= i) & (j >= i - look), 0.0, -1e30)
        a = np.tile(m[:, None, :], (1, NT, 1))
        a[0:BQ, ::TPB, 0:BQ] = -1e30
        return bf16_bits(a)

    c["mask_w"], c["mask_s"] = band(HD), band(32)
    c["ident"] = np.eye(P, dtype=f)
    c["shift"] = np.eye(P, k=1, dtype=f)
    e = np.zeros((P, P), f)
    e[P - 1, 0] = 1
    c["carry"] = e
    c["tri"] = bf16_bits(np.triu(np.ones((P, P), f), 1))
    c["ones"] = bf16_bits(np.ones((P, P), f))
    k = np.ones((P, NT), f)
    k[:, ::TPB] = 0
    c["keep"] = k
    pp = np.arange(P)
    c["rowmask"] = (pp[:, None] // LD == np.arange(LH)[None, :]).astype(f)
    c["tril"] = np.triu(np.ones((P, P), f))
    hh = np.arange(C) // LD
    c["blockm"] = (pp[:, None] // LD == hh[None, :]).astype(f)
    c["iota"] = bf16_bits(np.tile(np.arange(P, dtype=f), (P, 1)))
    c["iota4"] = np.tile(np.arange(SG, dtype=f), (P, 1))
    c["tokhi"] = np.tile(np.repeat(np.arange(NT, dtype=f), EX), (P, 1))
    c["toklo"] = np.tile(pp[:, None].astype(f), (1, NT * EX))
    s = np.ones((P, EX, NT), f)
    s[:, :, 0] = 0
    c["scanm"] = s.reshape(P, EX * NT)
    return c


def layout(i):
    import numpy as np

    a = {}
    a["x_in"] = i["L0_attn_x"].reshape(-1, C)
    a["wqkv"] = i["L0_ffn_wqkv"]
    a["qsc"], a["ksc"] = i["L0_ffn_q_scale"], i["L0_ffn_k_scale"]
    a["wo"] = i["L0_ffn_wo"]
    a["lng"], a["lnb"] = i["L0_ffn_ln_g"], i["L0_ffn_ln_b"]
    pad = HC * P - HID
    w1 = i["L0_ffn_w1"].reshape(DEPTH, C, 2, HID)
    a["w1"] = np.pad(w1, ((0, 0), (0, 0), (0, 0), (0, pad))).reshape(DEPTH, C, 2 * HC * P)
    b1 = np.pad(i["L0_ffn_b1"].reshape(DEPTH, 2, HID), ((0, 0), (0, 0), (0, pad)))
    a["b1"] = b1.reshape(DEPTH, 2 * HC, P).transpose(0, 2, 1)
    w2 = np.concatenate([i["L0_ffn_w2"], i["L0_ffn_b2"][:, None, :]], 1)
    a["w2"] = np.pad(w2, ((0, 0), (0, pad - 1), (0, 0)))
    a["awqkv"] = i["L0_attn_w_qkv"].T
    a["awout"] = i["L0_attn_w_out"].T
    a["lwqkv"] = np.concatenate([i["L1_attn_Wq"].T, i["L1_attn_Wk"].T, i["L1_attn_Wv"].T], 1)
    a["lwo"] = i["L1_attn_Wo"].T
    a["wg"] = i["L1_ffn_Wg"].T
    a["ew1"] = i["L1_ffn_W1"].transpose(0, 2, 1)
    a["ew3"] = i["L1_ffn_W3"].transpose(0, 2, 1)
    a["ew2"] = i["L1_ffn_W2"].transpose(0, 2, 1)
    return a


def kernel(**inputs):
    import numpy as np
    import concourse.bacc as bacc
    from concourse.bass_utils import run_bass_kernel_spmd as run

    given = {**layout({k: np.asarray(v) for k, v in inputs.items()}), **constants()}
    nc = bacc.Bacc("TRN2", target_bir_lowering=False, num_devices=1)
    arrays, args = {}, {}
    for name, a in given.items():
        a = np.ascontiguousarray(a)
        arrays["in_" + name] = a
        args[name] = nc.dram_tensor("in_" + name, a.shape, mybir.dt.from_np(a.dtype), kind="ExternalInput").ap()
        if a.dtype == np.uint16:
            args[name] = args[name].bitcast(BF16)
    out = nc.dram_tensor("out_x", (BATCH * SEQ, C), F32, kind="ExternalOutput").ap()
    bass_macaron(nc, out=out, **args)
    r = run(nc, [arrays], core_ids=[0])
    return r.results[0]["out_x"].reshape(BATCH, SEQ, C)
```
